# Optimizing a Trainium2 kernel written in Bass

```python
import numpy as np
import jax
import jax.numpy as jnp

def _softmax(x, axis=-1):
    return jax.nn.softmax(x, axis=axis)

def _gelu(x):
    return jax.nn.gelu(x, approximate=True)

def _silu(x):
    return jax.nn.silu(x)

def _sigmoid(x):
    return jax.nn.sigmoid(x)

def _layernorm(x, axis=-1, eps=1e-05):
    m = jnp.mean(x, axis=axis, keepdims=True)
    v = jnp.var(x, axis=axis, keepdims=True)
    return (x - m) / jnp.sqrt(v + eps)

def _scatter_add(tgt, idx, src, axis=0):
    return tgt.at[idx].add(src)

def _segment_sum(src, seg, n):
    return jax.ops.segment_sum(src, seg, n)
kernel_name = 'mk_cond_resid_d4_seqx_r2_c9856a'

def setup_inputs(seed: int=0):
    np.random.seed(seed)
    _w = jnp.asarray

    def _rec_inputs():
        import jax
        import jax.numpy as jnp
        _rk = jax.random.key(seed)
        x = -0.000125 + 0.9999 * jax.random.normal(jax.random.fold_in(_rk, 1), (4, 1024, 512), jnp.float32)
        _lenS = 1024 - jax.random.randint(jax.random.fold_in(_rk, 7), (4,), 0, max(1, 1024 // 4) + 1, jnp.int32)
        _lenS2 = 1024 - jax.random.randint(jax.random.fold_in(_rk, 8), (4,), 0, max(1, 1024 // 4) + 1, jnp.int32)
        itok_B_0_15 = jax.random.randint(jax.random.fold_in(_rk, 11), (4,), 0, 16, jnp.int32)
        itok_B_0_7 = jax.random.randint(jax.random.fold_in(_rk, 12), (4,), 0, 8, jnp.int32)
        condB_tauraws = -5.74692 + 0.777674 * jax.random.normal(jax.random.fold_in(_rk, 13), (4,), jnp.float32)
        cond_256 = -0.000235209 + 0.019331 * jax.random.normal(jax.random.fold_in(_rk, 14), (4, 128), jnp.float32)
        condB_bn2 = jnp.zeros((4,), jnp.float32)
        cond_1024 = -4.10585e-05 + 0.0199478 * jax.random.normal(jax.random.fold_in(_rk, 16), (4, 512), jnp.float32)
        return (x, itok_B_0_15, itok_B_0_7, condB_tauraws, cond_256, condB_bn2, cond_1024)
    x, itok_B_0_15, itok_B_0_7, condB_tauraws, cond_256, condB_bn2, cond_1024 = _rec_inputs()

    def _L0_cond_setup():
        import jax, jax.numpy as jnp
        import numpy as np
        B, N, DIM = (32, 512, 512)
        HID = 2048
        PART = 128
        OUT = 512
        SHARED = OUT - PART
        E = 16
        key = jax.random.key(seed)
        ks = jax.random.split(key, 8)
        s = 0.02
        return {'x': jax.random.normal(ks[0], (B, N, DIM), dtype=jnp.float32), 'indices': jax.random.randint(ks[1], (B,), 0, E, dtype=jnp.int64), 'fc1_w': jax.random.normal(ks[2], (HID, DIM), dtype=jnp.float32) * s, 'fc1_b': jnp.zeros((HID,), dtype=jnp.float32), 'fc2_w': jax.random.normal(ks[3], (SHARED, HID), dtype=jnp.float32) * s, 'fc2_b': jnp.zeros((SHARED,), dtype=jnp.float32), 'experts_w': jax.random.normal(ks[4], (E, PART, HID), dtype=jnp.float32) * s, 'experts_b': jnp.zeros((E, PART), dtype=jnp.float32)}
    _L0_cond_all = _L0_cond_setup()
    _L0_cond_in = {k: v for k, v in _L0_cond_all.items() if k in ('fc1_w', 'fc1_b', 'fc2_w', 'fc2_b', 'experts_w', 'experts_b')}
    del _L0_cond_all

    def _L1_cond_setup():
        import jax, jax.numpy as jnp
        import numpy as np
        S, O, H = (8, 512, 512)
        B, N = (32, 256)
        key = jax.random.key(seed)
        k1, k2, k3, k4 = jax.random.split(key, 4)
        x = jax.random.normal(k1, (B, N, H), dtype=jnp.float32)
        subject_id = jax.random.randint(k2, (B,), 0, S)
        wbound = jnp.sqrt(2.0 / 6.0) * jnp.sqrt(3.0 / H)
        weight = jax.random.uniform(k3, (S, O, H), minval=-wbound, maxval=wbound, dtype=jnp.float32)
        bbound = 1.0 / jnp.sqrt(H)
        bias = jax.random.uniform(k4, (S, O), minval=-bbound, maxval=bbound, dtype=jnp.float32)
        return {'x': x, 'subject_id': subject_id, 'weight': weight, 'bias': bias}
    _L1_cond_all = _L1_cond_setup()
    _L1_cond_in = {k: v for k, v in _L1_cond_all.items() if k in ('weight', 'bias')}
    del _L1_cond_all

    def _L2_cond_setup():
        import jax, jax.numpy as jnp
        import numpy as np
        import math
        B, T, E, D = (4, 1024, 512, 4)

        def _tau_init(t):
            a = 0.1 ** (1.0 / max(t - 1, 1))
            tt = -math.log(max(a, 1e-10))
            return math.log(math.exp(tt) - 1 + 1e-10)

        def causal_ema(b, tau_raw):
            alpha = jnp.exp(-jax.nn.softplus(tau_raw)).astype(b.dtype)

            def step(h, bt):
                h = alpha * h + bt
                return (h, h)
            h0 = jnp.zeros((b.shape[0], b.shape[2]), b.dtype)
            _, hs = jax.lax.scan(step, h0, jnp.swapaxes(b, 0, 1))
            return jnp.swapaxes(hs, 0, 1)
        key = jax.random.key(seed)
        ks = jax.random.split(key, 10)
        s = 0.02
        return {'x': jax.random.normal(ks[0], (B, T, E), jnp.float32), 'tau_ctx': jnp.float32(_tau_init(max(T // 2, 4))), 'tau_raws': jnp.array([_tau_init(max(T // 2 ** i, 2)) for i in range(D)], jnp.float32), 'Wg': jax.random.normal(ks[1], (E, 2 * E), jnp.float32) * s, 'bg': jnp.full((E,), -0.5, jnp.float32), 'Wn1': jax.random.normal(ks[2], (E // 4, E), jnp.float32) * s, 'bn1': jnp.zeros((E // 4,), jnp.float32), 'Wn2': jax.random.normal(ks[3], (D, E // 4), jnp.float32) * s, 'bn2': jnp.zeros((D,), jnp.float32), 'blend': jax.random.normal(ks[4], (D, E), jnp.float32) * s, 'Wsoma': jax.random.normal(ks[5], (E, E), jnp.float32) * s, 'bsoma': jnp.zeros((E,), jnp.float32), 'Wtemp': jax.random.normal(ks[6], (E, E), jnp.float32) * s, 'btemp': jnp.zeros((E,), jnp.float32), 'Wout': jax.random.normal(ks[7], (E, E), jnp.float32) * s, 'gamma': jnp.ones((E,), jnp.float32), 'beta': jnp.zeros((E,), jnp.float32)}
    _L2_cond_all = _L2_cond_setup()
    _L2_cond_in = {k: v for k, v in _L2_cond_all.items() if k in ('tau_ctx', 'Wg', 'bg', 'Wn1', 'bn1', 'Wsoma', 'bsoma', 'Wtemp', 'btemp', 'Wout', 'gamma', 'beta')}
    del _L2_cond_all

    def _L3_cond_setup():
        import jax, jax.numpy as jnp
        import numpy as np
        INPUT_DIM = 512
        OUTPUT_DIM = 512
        NUM_CATEGORIES = 16
        B, S = (32, 256)
        key = jax.random.key(seed)
        kx, kw, kb, ki = jax.random.split(key, 4)
        k = 1.0 / np.sqrt(INPUT_DIM)
        x = jax.random.normal(kx, (B, S, INPUT_DIM), dtype=jnp.float32)
        weight = jax.random.uniform(kw, (NUM_CATEGORIES, INPUT_DIM, OUTPUT_DIM), dtype=jnp.float32, minval=-k, maxval=k)
        bias = jax.random.uniform(kb, (NUM_CATEGORIES, OUTPUT_DIM), dtype=jnp.float32, minval=-k, maxval=k)
        emb_ids = jax.random.randint(ki, (B,), 0, NUM_CATEGORIES, dtype=jnp.int64)
        return {'x': x, 'emb_ids': emb_ids, 'weight': weight, 'bias': bias}
    _L3_cond_all = _L3_cond_setup()
    _L3_cond_in = {k: v for k, v in _L3_cond_all.items() if k in ('weight', 'bias')}
    del _L3_cond_all
    return {'x': x, 'itok_B_0_15': itok_B_0_15, 'itok_B_0_7': itok_B_0_7, 'condB_tauraws': condB_tauraws, 'cond_256': cond_256, 'condB_bn2': condB_bn2, 'cond_1024': cond_1024, 'L0_cond_fc1_w': _L0_cond_in['fc1_w'], 'L0_cond_fc1_b': _L0_cond_in['fc1_b'], 'L0_cond_fc2_w': _L0_cond_in['fc2_w'], 'L0_cond_fc2_b': _L0_cond_in['fc2_b'], 'L0_cond_experts_w': _L0_cond_in['experts_w'], 'L0_cond_experts_b': _L0_cond_in['experts_b'], 'L1_cond_weight': _L1_cond_in['weight'], 'L1_cond_bias': _L1_cond_in['bias'], 'L2_cond_tau_ctx': _L2_cond_in['tau_ctx'], 'L2_cond_Wg': _L2_cond_in['Wg'], 'L2_cond_bg': _L2_cond_in['bg'], 'L2_cond_Wn1': _L2_cond_in['Wn1'], 'L2_cond_bn1': _L2_cond_in['bn1'], 'L2_cond_Wsoma': _L2_cond_in['Wsoma'], 'L2_cond_bsoma': _L2_cond_in['bsoma'], 'L2_cond_Wtemp': _L2_cond_in['Wtemp'], 'L2_cond_btemp': _L2_cond_in['btemp'], 'L2_cond_Wout': _L2_cond_in['Wout'], 'L2_cond_gamma': _L2_cond_in['gamma'], 'L2_cond_beta': _L2_cond_in['beta'], 'L3_cond_weight': _L3_cond_in['weight'], 'L3_cond_bias': _L3_cond_in['bias']}

def reference(x, itok_B_0_15, itok_B_0_7, condB_tauraws, cond_256, condB_bn2, cond_1024, L0_cond_fc1_w, L0_cond_fc1_b, L0_cond_fc2_w, L0_cond_fc2_b, L0_cond_experts_w, L0_cond_experts_b, L1_cond_weight, L1_cond_bias, L2_cond_tau_ctx, L2_cond_Wg, L2_cond_bg, L2_cond_Wn1, L2_cond_bn1, L2_cond_Wsoma, L2_cond_bsoma, L2_cond_Wtemp, L2_cond_btemp, L2_cond_Wout, L2_cond_gamma, L2_cond_beta, L3_cond_weight, L3_cond_bias):
    import jax
    import jax.numpy as jnp

    def _L0_cond_ref(x, indices, fc1_w, fc1_b, fc2_w, fc2_b, experts_w, experts_b):
        import jax, jax.numpy as jnp
        import numpy as np
        B, N, DIM = (32, 512, 512)
        HID = 2048
        PART = 128
        OUT = 512
        SHARED = OUT - PART
        E = 16
        h = jax.nn.gelu(jnp.einsum('bnd,hd->bnh', x, fc1_w) + fc1_b, approximate=False)
        shared = jnp.einsum('bnh,sh->bns', h, fc2_w) + fc2_b
        We = experts_w[indices]
        be = experts_b[indices]
        expert_x = jnp.einsum('bnh,bph->bnp', h, We) + be[:, None, :]
        return jnp.concatenate([shared, expert_x], axis=-1)

    def _L1_cond_ref(x, subject_id, weight, bias):
        import jax, jax.numpy as jnp
        import numpy as np
        S, O, H = (8, 512, 512)
        B, N = (32, 256)
        W = weight[subject_id]
        b = bias[subject_id]
        y = jnp.einsum('bnh,boh->bno', x, W) + b[:, None, :]
        return y

    def _L2_cond_ref(x, tau_ctx, tau_raws, Wg, bg, Wn1, bn1, Wn2, bn2, blend, Wsoma, bsoma, Wtemp, btemp, Wout, gamma, beta):
        import jax, jax.numpy as jnp
        import numpy as np
        import math
        B, T, E, D = (4, 1024, 512, 4)

        def _tau_init(t):
            a = 0.1 ** (1.0 / max(t - 1, 1))
            tt = -math.log(max(a, 1e-10))
            return math.log(math.exp(tt) - 1 + 1e-10)

        def causal_ema(b, tau_raw):
            alpha = jnp.exp(-jax.nn.softplus(tau_raw)).astype(b.dtype)

            def step(h, bt):
                h = alpha * h + bt
                return (h, h)
            h0 = jnp.zeros((b.shape[0], b.shape[2]), b.dtype)
            _, hs = jax.lax.scan(step, h0, jnp.swapaxes(b, 0, 1))
            return jnp.swapaxes(hs, 0, 1)
        ctx = causal_ema(x, tau_ctx)
        gate_in = jnp.concatenate([x, ctx], axis=-1)
        wg = jax.nn.sigmoid(jnp.einsum('btc,ec->bte', gate_in, Wg) + bg)
        gated = x * wg
        h1 = jax.nn.gelu(jnp.einsum('btc,hc->bth', x, Wn1) + bn1, approximate=False)
        mod = 0.5 + jax.nn.sigmoid(jnp.einsum('bth,dh->btd', h1, Wn2) + bn2)
        traces = jax.vmap(lambda tau, m: causal_ema(gated * m[..., None], tau))(tau_raws, jnp.moveaxis(mod, -1, 0))
        blend_w = jax.nn.softmax(blend, axis=0)
        temporal = jnp.einsum('dbtc,dc->btc', traces, blend_w)
        gate = jax.nn.sigmoid(jnp.einsum('btc,ec->bte', temporal, Wtemp) + btemp)
        soma = jax.nn.gelu(jnp.einsum('btc,ec->bte', x, Wsoma) + bsoma, approximate=False)
        out = jnp.einsum('btc,ec->bte', soma * gate, Wout)
        mu = out.mean(-1, keepdims=True)
        var = out.var(-1, keepdims=True)
        return (out - mu) / jnp.sqrt(var + 1e-05) * gamma + beta

    def _L3_cond_ref(x, emb_ids, weight, bias):
        import jax, jax.numpy as jnp
        import numpy as np
        INPUT_DIM = 512
        OUTPUT_DIM = 512
        NUM_CATEGORIES = 16
        B, S = (32, 256)
        ids = emb_ids.reshape(-1).astype(jnp.int32)
        w = weight[ids]
        b = bias[ids]
        return jnp.einsum('bsi,bij->bsj', x, w) + b[:, None, :]
    x = x + _L0_cond_ref(x, itok_B_0_15, L0_cond_fc1_w, L0_cond_fc1_b, L0_cond_fc2_w, L0_cond_fc2_b, L0_cond_experts_w, L0_cond_experts_b)
    x = x + _L1_cond_ref(x, itok_B_0_7, L1_cond_weight, L1_cond_bias)
    x = x + _L2_cond_ref(x, L2_cond_tau_ctx, condB_tauraws, L2_cond_Wg, L2_cond_bg, L2_cond_Wn1, L2_cond_bn1, cond_256, condB_bn2, cond_1024, L2_cond_Wsoma, L2_cond_bsoma, L2_cond_Wtemp, L2_cond_btemp, L2_cond_Wout, L2_cond_gamma, L2_cond_beta)
    x = x + _L3_cond_ref(x, itok_B_0_15, L3_cond_weight, L3_cond_bias)
    return x

_drawn_inputs = setup_inputs


def setup_inputs(seed=0):
    import zlib

    import numpy as np

    out = dict(_drawn_inputs(seed))
    spreads = {'condB_bn2': (0.0, 2.0),
     'L0_cond_fc1_b': (0.0, 0.1),
     'L0_cond_fc2_b': (0.0, 0.1),
     'L0_cond_experts_b': (0.0, 0.1),
     'L2_cond_bg': (-0.5, 0.6),
     'L2_cond_bn1': (0.0, 2.0),
     'L2_cond_bsoma': (0.0, 0.1),
     'L2_cond_btemp': (0.0, 0.794),
     'L2_cond_gamma': (1.0, 0.2),
     'L2_cond_beta': (0.0, 0.1)}
    factors = {'condB_tauraws': 8.0,
     'cond_256': 8.0,
     'cond_1024': 24.949,
     'L2_cond_Wn1': 8.0,
     'L3_cond_bias': 3.974}
    for name, (base, spread) in spreads.items():
        noise = np.random.default_rng([zlib.crc32(name.encode()), seed]).standard_normal(out[name].shape)
        drawn = base * np.exp(spread * noise) if base else spread * noise
        out[name] = jnp.asarray(drawn.astype(out[name].dtype))
    for name, factor in factors.items():
        out[name] = (out[name] * factor).astype(out[name].dtype)
    return out
```

```python
import numpy as np
import concourse.bass as bass
from concourse import mybir
from contextlib import ExitStack

F32 = mybir.dt.float32
F32R = mybir.dt.float32r
I32 = mybir.dt.int32
ALU = mybir.AluOpType
ACT = mybir.ActivationFunctionType
AX = mybir.AxisListType

P = 128
B, SEQ, DIM = 4, 1024, 512
HID, EXPERTS, SUBJECTS = 2048, 16, 8
TAUS = 4
TOK = 512
HALVES = SEQ // TOK
NT = B * HALVES
KC = DIM // P
HC = HID // P
SH = KC - 1
KIB = 1024


def build(nc, x, tok16, tok8, fc1_w, fc2_w, exp_w, fc1_b, fc2_b, exp_b, l1_w, l1_b, taus, wg, bg,
          wn1, bn1, wn2, bn2, blend, wsoma, bsoma, wtemp, btemp, wout, gamma, beta, l3_w, l3_b, out):
    x1_dram = nc.dram_tensor("x1_dram", [NT, P, KC, TOK], F32, kind="Internal").ap()

    ctx = ExitStack()
    with ctx:
        base = (nc.sbuf_base + 63) // 64 * 64
        constants_at = [base + 200 * KIB]

        def place(name, kib, shape, dt=F32):
            return nc.alloc_sbuf_tensor_at(name, [P] + shape, dt, offset=base + int(kib * KIB))

        def const(name, n, dt=F32):
            at = constants_at[0]
            constants_at[0] += (4 * n + 31) // 32 * 32
            assert constants_at[0] <= nc.sbuf_usable_end
            return nc.alloc_sbuf_tensor_at(name, [P, n], dt, offset=at)

        def sem(name):
            return ctx.enter_context(nc.semaphore(name))

        NB = KC + SH + 1
        wa = place("wa", 0, [HC, 2, NB, P], F32R)
        x_hl = [place(f"x_hl{s}", 128 + 16 * s, [2, KC, TOK], F32R) for s in range(2)]
        x_raw = [place(f"x_raw{s}", 160 + 8 * s, [KC, TOK]) for s in range(2)]
        h_raw = [place(f"h_raw{s}", 176 + 2 * s, [TOK]) for s in range(2)]
        h_hl = [place(f"h_hl{s}", 180 + 4 * s, [2, TOK], F32R) for s in range(3)]
        w_stage = [place(f"w_stage{s}", 192 + 4 * s, [NB, P]) for s in range(2)]
        e_stage = place("e_stage", 192, [HC, P])
        l1w = [place("l1w0", 0, [KC, DIM]), place("l1w1", 64, [KC, DIM])]
        wn1_sb = place("wn1_sb", 8, [KC, P])
        wn2_rep = place("wn2_rep", 10, [TAUS, P])
        gated = [place(f"gated{s}", 12 + 2 * s, [TOK]) for s in range(2)]
        wsoma_sb = place("wsoma_sb", 16, [KC, DIM])
        wg_sb = place("wg_sb", 24, [2 * KC, DIM])
        wtemp_sb = place("wtemp_sb", 40, [KC, DIM])
        wout_sb = place("wout_sb", 48, [KC, DIM])
        l3w = [place("l3w0", 56, [KC, DIM]), place("l3w1", 72, [KC, DIM])]
        soma = [place(f"soma{s}", 80 + 8 * s, [KC, TOK]) for s in range(2)]
        temporal = [place(f"temporal{s}", 96 + 8 * s, [KC, TOK]) for s in range(2)]
        spikes = place("spikes", 112, [KC, TOK])
        o_sb = place("o_sb", 120, [KC, TOK])
        xt = [place(f"xt{s}", 128 + 8 * s, [KC, TOK]) for s in range(3)]
        ctx_sb = place("ctx_sb", 152, [KC, TOK])
        mod_t = place("mod_t", 160, [TAUS, TOK])
        wg_t = [place(f"wg_t{s}", 168 + 2 * s, [TOK]) for s in range(2)]
        drive = [place(f"drive{s}", 172 + 2 * s, [TOK]) for s in range(2)]
        trace = [place(f"trace{s}", 176 + 2 * s, [TOK]) for s in range(2)]
        gate_t = [place(f"gate_t{s}", 180 + 2 * s, [TOK]) for s in range(2)]
        square = [place(f"square{s}", 184 + 2 * s, [TOK]) for s in range(2)]
        sumsq = place("sumsq", 188, [TOK])
        std = place("std", 190, [TOK])
        rstd = place("rstd", 192, [TOK])
        h1 = place("h1", 194, [TOK])
        idx = const("idx", 2 * B, I32)
        fc1_b_sb = const("fc1_b_sb", HC)
        fc2_b_sb = const("fc2_b_sb", SH)
        exp_b_sb = const("exp_b_sb", B)
        l1_b_sb = const("l1_b_sb", B * KC)
        l3_b_sb = const("l3_b_sb", B * KC)
        tau_sb = const("tau_sb", 1 + TAUS)
        alpha = const("alpha", 1 + TAUS)
        bg_sb = const("bg_sb", KC)
        bn1_sb = const("bn1_sb", 1)
        wn2_sb = const("wn2_sb", TAUS)
        bn2_sb = const("bn2_sb", TAUS)
        blend_sb = const("blend_sb", KC * TAUS)
        blend_max = const("blend_max", KC)
        bsoma_sb = const("bsoma_sb", KC)
        btemp_sb = const("btemp_sb", KC)
        gamma_sb = const("gamma_sb", KC)
        beta_sb = const("beta_sb", KC)
        wout_mean = const("wout_mean", KC)
        eps_sb = const("eps_sb", 1)
        ctx_last = const("ctx_last", KC)
        trace_last = const("trace_last", KC * TAUS)
        ones = const("ones", P)

        bank = [ctx.enter_context(nc.psum_tensor(f"bank{i}", [P, TOK], F32)) for i in range(8)]
        acc = bank[0:KC]
        fc1_ring = bank[KC:8]

        s_idx = sem("s_idx")
        s_small = sem("s_small")
        s_wst = [sem(f"s_wst{s}") for s in range(2)]
        s_whi = sem("s_whi")
        s_wlo = sem("s_wlo")
        s_est = sem("s_est")
        s_ehi = sem("s_ehi")
        s_elo = sem("s_elo")
        s_xld = [sem(f"s_xld{s}") for s in range(2)]
        s_xhi = sem("s_xhi")
        s_xlo = sem("s_xlo")
        s_fc1 = sem("s_fc1")
        s_gelu = sem("s_gelu")
        s_hhi = sem("s_hhi")
        s_hlo = sem("s_hlo")
        s_fc2 = sem("s_fc2")
        s_x1 = sem("s_x1")
        s_x1st = sem("s_x1st")
        s_bw = {k: sem("s_bw_" + k) for k in ("l1", "n1", "soma", "g", "temp", "out", "l3")}
        s_xt = [sem(f"s_xt{s}") for s in range(3)]
        s_cst = sem("s_cst")
        s_blend_c = sem("s_blend_c")
        s_exp = sem("s_exp")
        s_wc = sem("s_wc")
        s_pe = {k: sem("s_pe_" + k) for k in
                ("L1", "N1", "SO", "MO", "WG", "TE", "OU", "SS", "L3")}
        s_x2 = sem("s_x2")
        s_ctx = sem("s_ctx")
        s_ctxl = sem("s_ctxl")
        s_h1 = sem("s_h1")
        s_soma = sem("s_soma")
        s_mod = sem("s_mod")
        s_wgt = sem("s_wgt")
        s_gated = sem("s_gated")
        s_drive = sem("s_drive")
        s_trace = sem("s_trace")
        s_tracel = sem("s_tracel")
        s_blend = sem("s_blend")
        s_gate = sem("s_gate")
        s_spk = sem("s_spk")
        s_o = sem("s_o")
        s_sq = sem("s_sq")
        s_ssq = sem("s_ssq")
        s_std = sem("s_std")
        s_rstd = sem("s_rstd")
        s_ln = sem("s_ln")
        s_x3 = sem("s_x3")
        s_y = sem("s_y")
        s_out = sem("s_out")

        class Waits:

            def __init__(self, eng):
                self.eng, self.seen = eng, {}

            def __call__(self, s, value):
                if value > self.seen.get(s.name, 0):
                    self.seen[s.name] = value
                    self.eng.wait_ge(s, value)

        CHUNKS = dict(L1=KC, N1=1, SO=KC, MO=TAUS, WG=KC, TE=KC, OU=KC, SS=1, L3=KC)
        LAG = dict(L1=0, SS=2, N1=0, SO=0, L3=2, MO=0, WG=0, TE=1, OU=1)
        ORDER = [(k, r - lag) for r in range(NT + 2) for k, lag in LAG.items() if 0 <= r - lag < NT]
        READ = dict(L1=s_x2, N1=s_h1, SO=s_soma, MO=s_mod, WG=s_wgt, TE=s_gate, OU=s_sq, SS=s_std, L3=s_y)
        slots = [(k, i, m) for k, i in ORDER for m in range(CHUNKS[k])]
        bank_of = {key: bank[n % 8] for n, key in enumerate(slots)}
        before = {key: slots[n - 8] if n >= 8 else None for n, key in enumerate(slots)}
        last_fc2 = NT * HC
        V_ORDER = []
        for r in range(NT + 2):
            steps = [("L1", r, 0), ("SS", r - 2, 0), ("L3", r - 2, 0), ("WG", r, 0), ("WG", r, 1),
                     ("WG", r, 2), ("TE", r - 1, 0), ("WG", r, 3), ("OU", r - 1, 0)]
            V_ORDER += [s for s in steps if 0 <= s[1] < NT]

        block = ctx.enter_context(nc.Block())

        @block.sync
        def _(eng):
            wait = Waits(eng)
            eng.dma_start(idx[0:1, 0:B], tok16).then_inc(s_idx, 16)
            eng.dma_start(idx[0:1, B:2 * B], tok8).then_inc(s_idx, 16)
            eng.dma_start(x_raw[0][:, :, :], x[0]).then_inc(s_xld[0], 16)
            wait(s_idx, 32)
            expert = [nc.sync.value_load(idx[0:1, b:b + 1], min_val=0, max_val=EXPERTS - 1) for b in range(B)]
            subject = [nc.sync.value_load(idx[0:1, B + b:B + b + 1], min_val=0, max_val=SUBJECTS - 1)
                       for b in range(B)]

            def load_weights(j):
                if j >= 2:
                    wait(s_wlo, j - 1)
                st = w_stage[j % 2]
                eng.dma_start(st[:, 0:KC, :], fc1_w[j]).then_inc(s_wst[j % 2], 16)
                eng.dma_start(st[:, KC:KC + SH, :], fc2_w[j]).then_inc(s_wst[j % 2], 16)
                eng.dma_start(st[:, NB - 1:NB, :],
                              exp_w[bass.ds(expert[0], 1), :, j:j + 1, :].rearrange("e p a n -> p (e a) n")
                              ).then_inc(s_wst[j % 2], 16)

            load_weights(0)
            load_weights(1)
            small = [(fc1_b_sb, fc1_b), (fc2_b_sb, fc2_b), (tau_sb, taus), (bg_sb, bg), (bn1_sb, bn1),
                     (wn2_sb, wn2), (bn2_sb, bn2), (blend_sb, blend), (bsoma_sb, bsoma),
                     (btemp_sb, btemp), (gamma_sb, gamma), (beta_sb, beta)]
            for dst, src in small:
                eng.dma_start(dst[:, :], src).then_inc(s_small, 16)
            for b in range(B):
                eng.dma_start(exp_b_sb[:, b:b + 1], exp_b[bass.ds(expert[b], 1), :].rearrange("e p -> p e")
                              ).then_inc(s_small, 16)
                eng.dma_start(l1_b_sb[:, b * KC:(b + 1) * KC],
                              l1_b[bass.ds(subject[b], 1), :, :].rearrange("e p c -> p (e c)")
                              ).then_inc(s_small, 16)
                eng.dma_start(l3_b_sb[:, b * KC:(b + 1) * KC],
                              l3_b[bass.ds(expert[b], 1), :, :].rearrange("e p c -> p (e c)")
                              ).then_inc(s_small, 16)
            for j in range(2, HC):
                load_weights(j)
                if j == 4:
                    eng.dma_start(x_raw[1][:, :, :], x[1]).then_inc(s_xld[1], 16)
            for t in range(NT - 1):
                b = t // HALVES
                if t % HALVES == 0 and b + 1 < B:
                    wait(s_wlo, HC)
                    wait(s_elo, HC * b)
                    eng.dma_start(e_stage[:, :, :],
                                  exp_w[bass.ds(expert[b + 1], 1), :, :, :].rearrange("e p a n -> p (e a) n")
                                  ).then_inc(s_est, 16)
                wait(s_x1, KC * (t + 1))
                eng.dma_start(x1_dram[t], x_raw[t % 2][:, :, :]).then_inc(s_x1st, 16)
                if t + 2 < NT:
                    wait(s_x1st, 16 * (t + 1))
                    eng.dma_start(x_raw[t % 2][:, :, :], x[t + 2]).then_inc(s_xld[t % 2], 16)

            def load_l1(b):
                eng.dma_start(l1w[b % 2][:, :, :],
                              l1_w[bass.ds(subject[b], 1), :, :, :].rearrange("e p c n -> p (e c) n")
                              ).then_inc(s_bw["l1"], 16)

            def load_l3(b):
                eng.dma_start(l3w[b % 2][:, :, :],
                              l3_w[bass.ds(expert[b], 1), :, :, :].rearrange("e p c n -> p (e c) n")
                              ).then_inc(s_bw["l3"], 16)

            def chunk_left(j):
                wait(s_fc2, (NT - 1) * HC + j + 1)

            def load_xt(i):
                eng.dma_start(xt[i % 3][:, :, :], x1_dram[i]).then_inc(s_xt[i % 3], 16)

            wait(s_x1st, 16 * 2)
            wait(s_fc1, (NT - 1) * HC)
            load_xt(0)
            load_xt(1)
            chunk_left(0)
            load_l1(0)
            chunk_left(1)
            eng.dma_start(wn1_sb[:, :, :], wn1).then_inc(s_bw["n1"], 16)
            chunk_left(2)
            eng.dma_start(wsoma_sb[:, :, :], wsoma).then_inc(s_bw["soma"], 16)
            chunk_left(4)
            eng.dma_start(wg_sb[:, :, :], wg).then_inc(s_bw["g"], 16)
            chunk_left(5)
            eng.dma_start(wtemp_sb[:, :, :], wtemp).then_inc(s_bw["temp"], 16)
            chunk_left(6)
            eng.dma_start(wout_sb[:, :, :], wout).then_inc(s_bw["out"], 16)
            chunk_left(7)
            load_l3(0)
            wait(s_x1, KC * NT)
            eng.dma_start(x1_dram[NT - 1], x_raw[(NT - 1) % 2][:, :, :]).then_inc(s_x1st, 16)
            wait(s_x1st, 16 * NT)
            wait(s_fc2, last_fc2)
            load_xt(2)
            wait(s_bw["l1"], 16)
            load_l1(1)
            wait(s_bw["l3"], 16)
            load_l3(1)
            for i in range(NT):
                b = i // HALVES
                wait(s_y, KC * (i + 1))
                eng.dma_start(out[i], o_sb[:, :, :]).then_inc(s_out, 16)
                if i + 3 < NT:
                    load_xt(i + 3)
                if i % HALVES == HALVES - 1 and b + 2 < B:
                    wait(s_pe["L1"], KC * HALVES * (b + 1))
                    wait(s_bw["l1"], 16 * (b + 2))
                    load_l1(b + 2)
                    wait(s_pe["L3"], KC * HALVES * (b + 1))
                    wait(s_bw["l3"], 16 * (b + 2))
                    load_l3(b + 2)
            wait(s_out, 16 * NT)

        @block.scalar
        def _(eng):
            wait = Waits(eng)
            n_small = 16 * (12 + 3 * B)

            def w_hi(j):
                wait(s_wst[j % 2], 48 * (j // 2 + 1))
                eng.activation(wa[:, j, 0, :, :], w_stage[j % 2][:, :, :], ACT.Copy).then_inc(s_whi, 1)

            def x_hi(t, c):
                wait(s_xld[t % 2], 16 * (t // 2 + 1))
                if t >= 2:
                    wait(s_fc1, HC * (t - 1))
                eng.activation(x_hl[t % 2][:, 0, c, :], x_raw[t % 2][:, c, :], ACT.Copy).then_inc(s_xhi, 1)

            for c in range(KC):
                x_hi(0, c)
            w_hi(0)
            w_hi(1)
            wait(s_small, n_small)
            eng.activation(alpha[:, :], tau_sb[:, :], ACT.Exp).then_inc(s_exp, 1)
            wait(s_cst, 2)
            eng.activation(blend_sb[:, :], blend_sb[:, :], ACT.Exp).then_inc(s_exp, 1)
            for u in range(NT * HC):
                t, j = divmod(u, HC)
                if t == 0 and j + 2 < HC:
                    w_hi(j + 2)
                wait(s_fc1, u + 1)
                if u >= 2:
                    wait(s_hlo, u - 1)
                eng.activation(h_raw[u % 2][:, :], fc1_ring[u % 4][:, :], ACT.Gelu,
                               bias=fc1_b_sb[:, j:j + 1]).then_inc(s_gelu, 1)
                wait(s_gelu, u + 1)
                if u >= 3:
                    wait(s_fc2, u - 2)
                eng.activation(h_hl[u % 3][:, 0, :], h_raw[u % 2][:, :], ACT.Copy).then_inc(s_hhi, 1)
                if 4 <= j < 4 + KC and t + 1 < NT:
                    x_hi(t + 1, j - 4)
                v = u - 4
                if v >= 0 and (v // HC) % HALVES == HALVES - 1 and v // HC < NT - 1:
                    b, je = v // HC // HALVES, v % HC
                    wait(s_est, 16 * (b + 1))
                    wait(s_fc2, v + 1)
                    eng.activation(wa[:, je, 0, NB - 1, :], e_stage[:, je, :], ACT.Copy).then_inc(s_ehi, 1)

            wait(s_x1st, 16 * NT)
            for k, i in ORDER:
                for m in range(CHUNKS[k]):
                    ps, n = bank_of[k, i, m], CHUNKS[k] * i + m
                    if k in ("L1", "L3"):
                        continue
                    wait(s_pe[k], n + 1)
                    if k == "N1":
                        if i:
                            wait(s_pe["MO"], TAUS * i)
                        eng.activation(h1[:, :], ps[:, :], ACT.Gelu, bias=bn1_sb[:, 0:1]).then_inc(s_h1, 1)
                    elif k == "SO":
                        if i >= 2:
                            wait(s_spk, KC * (i - 2) + m + 1)
                        eng.activation(soma[i % 2][:, m, :], ps[:, :], ACT.Gelu,
                                       bias=bsoma_sb[:, m:m + 1]).then_inc(s_soma, 1)
                    elif k == "MO":
                        if i:
                            wait(s_drive, KC * TAUS * i)
                        eng.activation(mod_t[:, m, :], ps[:, :], ACT.Tanh, bias=bn2_sb[:, m:m + 1],
                                       scale=0.5).then_inc(s_mod, 1)
                    elif k == "WG":
                        if n >= 2:
                            wait(s_gated, n - 1)
                        eng.activation(wg_t[n % 2][:, :], ps[:, :], ACT.Tanh, bias=bg_sb[:, m:m + 1],
                                       scale=0.5).then_inc(s_wgt, 1)
                    elif k == "TE":
                        if n >= 2:
                            wait(s_spk, n - 1)
                        eng.activation(gate_t[n % 2][:, :], ps[:, :], ACT.Tanh, bias=btemp_sb[:, m:m + 1],
                                       scale=0.5).then_inc(s_gate, 1)
                    elif k == "OU":
                        if i:
                            wait(s_out, 16 * i)
                        eng.activation(o_sb[:, m, :], ps[:, :], ACT.Copy).then_inc(s_o, 1)
                        if n >= 2:
                            wait(s_ssq, n - 1)
                        eng.activation(square[n % 2][:, :], ps[:, :], ACT.Square).then_inc(s_sq, 1)
                    elif k == "SS":
                        if i:
                            wait(s_rstd, i)
                        eng.activation(std[:, :], ps[:, :], ACT.Sqrt, bias=eps_sb[:, 0:1],
                                       scale=1.0 / DIM).then_inc(s_std, 1)

        @block.tensor
        def _(eng):
            wait = Waits(eng)

            def split_product(ps, w_hi, w_lo, x_hi, x_lo, first, last):
                eng.matmul(ps, w_hi, x_hi, start=first, stop=False)
                eng.matmul(ps, w_hi, x_lo, start=False, stop=False)
                return eng.matmul(ps, w_lo, x_hi, start=False, stop=last)

            def fc1(u):
                t, j = divmod(u, HC)
                wait(s_wlo, j + 1)
                wait(s_xlo, KC * (t + 1))
                if u >= 4:
                    wait(s_gelu, u - 3)
                for c in range(KC):
                    mm = split_product(fc1_ring[u % 4][:, :], wa[:, j, 0, c, :], wa[:, j, 1, c, :],
                                       x_hl[t % 2][:, 0, c, :], x_hl[t % 2][:, 1, c, :], c == 0, c == KC - 1)
                mm.then_inc(s_fc1, 1)

            def fc2(u):
                t, j = divmod(u, HC)
                wait(s_hlo, u + 1)
                b = t // HALVES
                if b:
                    wait(s_elo, HC * (b - 1) + j + 1)
                if j == 0 and t:
                    wait(s_x1, KC * t)
                for m in range(KC):
                    mm = split_product(acc[m][:, :], wa[:, j, 0, KC + m, :], wa[:, j, 1, KC + m, :],
                                       h_hl[u % 3][:, 0, :], h_hl[u % 3][:, 1, :], j == 0, j == HC - 1)
                mm.then_inc(s_fc2, 1)

            for u in range(NT * HC + 2):
                if u < NT * HC:
                    fc1(u)
                if u >= 2:
                    fc2(u - 2)

            wait(s_x1, KC * NT)
            wait(s_gelu, NT * HC)
            for k, i in ORDER:
                b = i // HALVES
                for m in range(CHUNKS[k]):
                    ps = bank_of[k, i, m]
                    if before[k, i, m]:
                        bk, bi, bm = before[k, i, m]
                        wait(READ[bk], CHUNKS[bk] * bi + bm + 1)
                    cols = slice(m * P, (m + 1) * P)
                    x2 = [xt[i % 3][:, c, :] for c in range(KC)]
                    if k == "L1":
                        wait(s_bw["l1"], 16 * (b + 1))
                        wait(s_xt[i % 3], 16 * (i // 3 + 1))
                        terms = [(l1w[b % 2][:, c, cols], x2[c]) for c in range(KC)]
                    elif k == "N1":
                        wait(s_bw["n1"], 16)
                        wait(s_x2, KC * (i + 1))
                        terms = [(wn1_sb[:, c, :], x2[c]) for c in range(KC)]
                    elif k == "SO":
                        wait(s_bw["soma"], 16)
                        terms = [(wsoma_sb[:, c, cols], x2[c]) for c in range(KC)]
                    elif k == "MO":
                        wait(s_wc, 1)
                        wait(s_h1, i + 1)
                        terms = [(wn2_rep[:, m, :], h1[:, :])]
                    elif k == "WG":
                        wait(s_bw["g"], 16)
                        wait(s_ctx, KC * (i + 1))
                        terms = [(wg_sb[:, c, cols], x2[c]) for c in range(KC)]
                        terms += [(wg_sb[:, KC + c, cols], ctx_sb[:, c, :]) for c in range(KC)]
                    elif k == "TE":
                        wait(s_bw["temp"], 16)
                        wait(s_blend, TAUS * KC * (i + 1))
                        terms = [(wtemp_sb[:, c, cols], temporal[i % 2][:, c, :]) for c in range(KC)]
                    elif k == "OU":
                        wait(s_wc, 3 + KC)
                        wait(s_spk, KC * (i + 1))
                        terms = [(wout_sb[:, c, cols], spikes[:, c, :]) for c in range(KC)]
                    elif k == "SS":
                        wait(s_cst, 1)
                        wait(s_ssq, KC * (i + 1))
                        terms = [(ones[:, :], sumsq[:, :])]
                    elif k == "L3":
                        wait(s_bw["l3"], 16 * (b + 1))
                        wait(s_x3, KC * (i + 1))
                        terms = [(l3w[b % 2][:, c, cols], x2[c]) for c in range(KC)]
                    for n, (w, r) in enumerate(terms):
                        mm = eng.matmul(ps[:, :], w, r, start=n == 0, stop=n == len(terms) - 1)
                    mm.then_inc(s_pe[k], 1)

        @block.vector
        def _(eng):
            wait = Waits(eng)

            def w_lo(j):
                wait(s_whi, j + 1)
                eng.tensor_tensor(wa[:, j, 1, :, :], w_stage[j % 2][:, :, :], wa[:, j, 0, :, :].bitcast(F32),
                                  ALU.subtract).then_inc(s_wlo, 1)

            def x_lo(t, c):
                wait(s_xhi, KC * t + c + 1)
                eng.tensor_tensor(x_hl[t % 2][:, 1, c, :], x_raw[t % 2][:, c, :],
                                  x_hl[t % 2][:, 0, c, :].bitcast(F32), ALU.subtract).then_inc(s_xlo, 1)

            for c in range(KC):
                x_lo(0, c)
            w_lo(0)
            w_lo(1)
            n_small = 16 * (12 + 3 * B)
            eng.memset(ones[:, :], 1.0)
            eng.memset(eps_sb[:, :], 1e-5).then_inc(s_cst, 1)
            wait(s_small, n_small)
            eng.tensor_scalar(bg_sb[:, :], bg_sb[:, :], 0.5, None, ALU.mult)
            eng.tensor_scalar(bn2_sb[:, :], bn2_sb[:, :], 0.5, None, ALU.mult)
            eng.tensor_scalar(btemp_sb[:, :], btemp_sb[:, :], 0.5, None, ALU.mult)
            blend_v = blend_sb[:, :].rearrange("p (c d) -> p c d", d=TAUS)
            links = [0]

            def link(ins):
                links[0] += 1
                ins.then_inc(s_blend_c, 1)
                wait(s_blend_c, links[0])

            link(eng.tensor_reduce(blend_max[:, :], blend_v, AX.X, ALU.max))
            for c in range(KC):
                ins = eng.tensor_scalar(blend_v[:, c, :], blend_v[:, c, :], blend_max[:, c:c + 1], None,
                                        ALU.subtract)
            ins.then_inc(s_cst, 1)
            wait(s_exp, 2)
            link(eng.tensor_reduce(blend_max[:, :], blend_v, AX.X, ALU.add))
            link(eng.reciprocal(blend_max[:, :], blend_max[:, :]))
            for c in range(KC):
                eng.tensor_scalar(blend_v[:, c, :], blend_v[:, c, :], blend_max[:, c:c + 1], 0.25,
                                  ALU.mult, ALU.mult)
            link(eng.tensor_scalar(alpha[:, :], alpha[:, :], 1.0, None, ALU.add))
            link(eng.reciprocal(alpha[:, :], alpha[:, :]))

            for u in range(NT * HC + 2):
                t, j = divmod(u, HC)
                if t == 0 and j + 2 < HC:
                    w_lo(j + 2)
                if u < NT * HC:
                    wait(s_hhi, u + 1)
                    if u >= 3:
                        wait(s_fc2, u - 2)
                    eng.tensor_tensor(h_hl[u % 3][:, 1, :], h_raw[u % 2][:, :],
                                      h_hl[u % 3][:, 0, :].bitcast(F32), ALU.subtract).then_inc(s_hlo, 1)
                if t and j == 1:
                    wait(s_fc2, HC * t)
                    for m in range(KC):
                        eb = (t - 1) // HALVES
                        bias = fc2_b_sb[:, m:m + 1] if m < SH else exp_b_sb[:, eb:eb + 1]
                        xr = x_raw[(t - 1) % 2][:, m, :]
                        eng.scalar_tensor_tensor(xr, acc[m][:, :], bias, xr, ALU.add, ALU.add
                                                 ).then_inc(s_x1, 1)
                if 4 <= j < 4 + KC and t + 1 < NT:
                    x_lo(t + 1, j - 4)
                v = u - 4
                if v >= 0 and (v // HC) % HALVES == HALVES - 1 and v // HC < NT - 1:
                    b, je = v // HC // HALVES, v % HC
                    wait(s_ehi, HC * b + je + 1)
                    eng.tensor_tensor(wa[:, je, 1, NB - 1, :], e_stage[:, je, :],
                                      wa[:, je, 0, NB - 1, :].bitcast(F32), ALU.subtract).then_inc(s_elo, 1)

            wait(s_fc2, (NT - 1) * HC + 2)
            for d in range(TAUS):
                ins = eng.tensor_copy(wn2_rep[:, d, :], wn2_sb[:, d:d + 1].to_broadcast([P, P]))
            ins.then_inc(s_wc, 1)
            wait(s_bw["out"], 16)
            eng.tensor_reduce(wout_mean[:, :], wout_sb[:, :, :], AX.X, ALU.add).then_inc(s_wc, 1)
            wait(s_wc, 2)
            eng.tensor_scalar(wout_mean[:, :], wout_mean[:, :], 1.0 / DIM, None, ALU.mult).then_inc(s_wc, 1)
            wait(s_wc, 3)
            for c in range(KC):
                eng.tensor_scalar(wout_sb[:, c, :], wout_sb[:, c, :], wout_mean[:, c:c + 1], 0.5,
                                  ALU.subtract, ALU.mult).then_inc(s_wc, 1)
            wait(s_x1st, 16 * NT)

            def add_squares(i):
                for m in range(KC):
                    n = KC * i + m
                    wait(s_sq, n + 1)
                    if m == 0:
                        if i:
                            wait(s_pe["SS"], i)
                        eng.tensor_copy(sumsq[:, :], square[n % 2][:, :]).then_inc(s_ssq, 1)
                    else:
                        wait(s_ssq, n)
                        eng.tensor_tensor(sumsq[:, :], sumsq[:, :], square[n % 2][:, :], ALU.add
                                          ).then_inc(s_ssq, 1)

            for k, i, part in V_ORDER:
                b = i // HALVES
                x2 = xt[i % 3]
                first_half = i % HALVES == 0
                if k == "L1":
                    for m in range(KC):
                        wait(s_pe["L1"], KC * (i + 1))
                        eng.scalar_tensor_tensor(x2[:, m, :], bank_of[k, i, m][:, :],
                                                 l1_b_sb[:, b * KC + m:b * KC + m + 1], x2[:, m, :],
                                                 ALU.add, ALU.add).then_inc(s_x2, 1)
                    for c in range(KC):
                        wait(s_x2, KC * i + c + 1)
                        if i:
                            wait(s_pe["WG"], KC * i)
                        if first_half:
                            start = 0.0
                        else:
                            wait(s_ctxl, KC * (i // HALVES) + c + 1)
                            start = ctx_last[:, c:c + 1]
                        eng.tensor_tensor_scan(ctx_sb[:, c, :], alpha[:, 0:1].to_broadcast([P, TOK]),
                                               x2[:, c, :], start, ALU.mult, ALU.add).then_inc(s_ctx, 1)
                    if first_half:
                        wait(s_ctx, KC * (i + 1))
                        for c in range(KC):
                            eng.tensor_copy(ctx_last[:, c:c + 1], ctx_sb[:, c, TOK - 1:TOK]).then_inc(s_ctxl, 1)
                elif k == "WG":
                    for c in [part]:
                        n = KC * i + c
                        wait(s_wgt, n + 1)
                        g = gated[n % 2]
                        if n >= 2:
                            wait(s_drive, TAUS * (n - 1))
                        eng.scalar_tensor_tensor(g[:, :], wg_t[n % 2][:, :], 1.0, x2[:, c, :],
                                                 ALU.add, ALU.mult).then_inc(s_gated, 1)
                        wait(s_gated, n + 1)
                        wait(s_mod, TAUS * (i + 1))

                        def drive_of(d):
                            q = TAUS * n + d
                            if q >= 2:
                                wait(s_trace, q - 1)
                            eng.scalar_tensor_tensor(drive[q % 2][:, :], mod_t[:, d, :], 2.0, g[:, :],
                                                     ALU.add, ALU.mult).then_inc(s_drive, 1)

                        def trace_of(d):
                            q = TAUS * n + d
                            wait(s_drive, q + 1)
                            if q >= 2:
                                wait(s_blend, q - 1)
                            if first_half:
                                start = 0.0
                            else:
                                wait(s_tracel, TAUS * KC * (i // HALVES) + TAUS * c + d + 1)
                                start = trace_last[:, TAUS * c + d:TAUS * c + d + 1]
                            eng.tensor_tensor_scan(trace[q % 2][:, :],
                                                   alpha[:, 1 + d:2 + d].to_broadcast([P, TOK]),
                                                   drive[q % 2][:, :], start, ALU.mult, ALU.add
                                                   ).then_inc(s_trace, 1)

                        def blend_of(d):
                            q = TAUS * n + d
                            wait(s_trace, q + 1)
                            tr, te = trace[q % 2], temporal[i % 2][:, c, :]
                            if first_half:
                                eng.tensor_copy(trace_last[:, TAUS * c + d:TAUS * c + d + 1],
                                                tr[:, TOK - 1:TOK]).then_inc(s_tracel, 1)
                            w = blend_sb[:, TAUS * c + d:TAUS * c + d + 1]
                            if d == 0:
                                if i >= 2:
                                    wait(s_pe["TE"], KC * (i - 1))
                                eng.tensor_scalar(te, tr[:, :], w, None, ALU.mult).then_inc(s_blend, 1)
                            else:
                                wait(s_blend, q)
                                eng.scalar_tensor_tensor(te, tr[:, :], w, te, ALU.mult, ALU.add
                                                         ).then_inc(s_blend, 1)

                        drive_of(0)
                        drive_of(1)
                        trace_of(0)
                        for d in range(1, TAUS):
                            if d + 1 < TAUS:
                                drive_of(d + 1)
                            blend_of(d - 1)
                            trace_of(d)
                        blend_of(TAUS - 1)
                elif k == "TE":
                    for m in range(KC):
                        n = KC * i + m
                        wait(s_gate, n + 1)
                        wait(s_soma, n + 1)
                        if i:
                            wait(s_pe["OU"], KC * i)
                        eng.scalar_tensor_tensor(spikes[:, m, :], gate_t[n % 2][:, :], 1.0,
                                                 soma[i % 2][:, m, :], ALU.add, ALU.mult).then_inc(s_spk, 1)
                elif k == "OU":
                    add_squares(i)
                elif k == "SS":
                    wait(s_std, i + 1)
                    if i:
                        wait(s_ln, KC * i)
                    eng.reciprocal(rstd[:, :], std[:, :]).then_inc(s_rstd, 1)
                    wait(s_rstd, i + 1)
                    wait(s_o, KC * (i + 1))
                    for m in range(KC):
                        eng.scalar_tensor_tensor(o_sb[:, m, :], o_sb[:, m, :], gamma_sb[:, m:m + 1],
                                                 rstd[:, :], ALU.mult, ALU.mult).then_inc(s_ln, 1)
                    for m in range(KC):
                        wait(s_ln, KC * i + m + 1)
                        eng.scalar_tensor_tensor(x2[:, m, :], o_sb[:, m, :], beta_sb[:, m:m + 1],
                                                 x2[:, m, :], ALU.add, ALU.add).then_inc(s_x3, 1)
                elif k == "L3":
                    for m in range(KC):
                        wait(s_pe["L3"], KC * i + m + 1)
                        wait(s_x3, KC * (i + 1))
                        eng.scalar_tensor_tensor(o_sb[:, m, :], bank_of[k, i, m][:, :],
                                                 l3_b_sb[:, b * KC + m:b * KC + m + 1], x2[:, m, :],
                                                 ALU.add, ALU.add).then_inc(s_y, 1)


def kernel(x, itok_B_0_15, itok_B_0_7, condB_tauraws, cond_256, condB_bn2, cond_1024, L0_cond_fc1_w,
           L0_cond_fc1_b, L0_cond_fc2_w, L0_cond_fc2_b, L0_cond_experts_w, L0_cond_experts_b,
           L1_cond_weight, L1_cond_bias, L2_cond_tau_ctx, L2_cond_Wg, L2_cond_bg, L2_cond_Wn1,
           L2_cond_bn1, L2_cond_Wsoma, L2_cond_bsoma, L2_cond_Wtemp, L2_cond_btemp, L2_cond_Wout,
           L2_cond_gamma, L2_cond_beta, L3_cond_weight, L3_cond_bias):
    import concourse.bacc as bacc
    from concourse.bass_utils import run_bass_kernel_spmd

    def a(v):
        return np.asarray(v)

    def stationary(w):
        o, i = w.shape
        return w.T.reshape(i // P, P, o).transpose(1, 0, 2)

    def columns(v):
        return v.reshape(-1, P).T

    data = {
        "x": a(x).reshape(B, HALVES, TOK, KC, P).transpose(0, 1, 4, 3, 2).reshape(NT, P, KC, TOK),
        "tok16": a(itok_B_0_15).reshape(1, B),
        "tok8": a(itok_B_0_7).reshape(1, B),
        "fc1_w": a(L0_cond_fc1_w).reshape(HC, P, KC, P).transpose(0, 3, 2, 1),
        "fc2_w": a(L0_cond_fc2_w).T.reshape(HC, P, SH, P),
        "exp_w": a(L0_cond_experts_w).reshape(EXPERTS, P, HC, P).transpose(0, 3, 2, 1),
        "fc1_b": columns(a(L0_cond_fc1_b)),
        "fc2_b": columns(a(L0_cond_fc2_b)),
        "exp_b": a(L0_cond_experts_b),
        "l1_w": a(L1_cond_weight).transpose(0, 2, 1).reshape(SUBJECTS, KC, P, DIM).transpose(0, 2, 1, 3),
        "l1_b": a(L1_cond_bias).reshape(SUBJECTS, KC, P).transpose(0, 2, 1),
        "taus": np.broadcast_to(np.concatenate([a(L2_cond_tau_ctx).reshape(1), a(condB_tauraws)]), (P, 1 + TAUS)),
        "wg": stationary(a(L2_cond_Wg)),
        "bg": columns(a(L2_cond_bg)),
        "wn1": stationary(a(L2_cond_Wn1)),
        "bn1": columns(a(L2_cond_bn1)),
        "wn2": a(cond_256).T,
        "bn2": np.broadcast_to(a(condB_bn2), (P, TAUS)),
        "blend": a(cond_1024).reshape(TAUS, KC, P).transpose(2, 1, 0).reshape(P, KC * TAUS),
        "wsoma": stationary(a(L2_cond_Wsoma)),
        "bsoma": columns(a(L2_cond_bsoma)),
        "wtemp": stationary(a(L2_cond_Wtemp)),
        "btemp": columns(a(L2_cond_btemp)),
        "wout": stationary(a(L2_cond_Wout)),
        "gamma": columns(a(L2_cond_gamma)),
        "beta": columns(a(L2_cond_beta)),
        "l3_w": a(L3_cond_weight).reshape(EXPERTS, KC, P, DIM).transpose(0, 2, 1, 3),
        "l3_b": a(L3_cond_bias).reshape(EXPERTS, KC, P).transpose(0, 2, 1),
    }
    nc = bacc.Bacc("TRN2", target_bir_lowering=False, num_devices=1)
    arrays, args = {}, []
    for name, v in data.items():
        arrays["in_" + name] = np.ascontiguousarray(v)
        args.append(nc.dram_tensor("in_" + name, v.shape, mybir.dt.from_np(v.dtype), kind="ExternalInput").ap())
    args.append(nc.dram_tensor("out", [NT, P, KC, TOK], F32, kind="ExternalOutput").ap())
    build(nc, *args)
    r = run_bass_kernel_spmd(nc, [arrays], core_ids=[0])
    y = r.results[0]["out"]
    return y.reshape(B, HALVES, P, KC, TOK).transpose(0, 1, 4, 3, 2).reshape(B, SEQ, DIM)
```

```python
import numpy as np
import concourse.bass as bass
from concourse import mybir
from contextlib import ExitStack

F32 = mybir.dt.float32
F32R = mybir.dt.float32r
I32 = mybir.dt.int32
ALU = mybir.AluOpType
ACT = mybir.ActivationFunctionType
AX = mybir.AxisListType

P = 128
B, SEQ, DIM = 4, 1024, 512
HID, EXPERTS, SUBJECTS = 2048, 16, 8
TAUS = 4
TOK = 512
HALVES = SEQ // TOK
NT = B * HALVES
KC = DIM // P
HC = HID // P
SH = KC - 1
KIB = 1024


def build(nc, x, tok16, tok8, fc1_w, fc2_w, exp_w, fc1_b, fc2_b, exp_b, l1_w, l1_b, taus, wg, bg,
          wn1, bn1, wn2, bn2, blend, wsoma, bsoma, wtemp, btemp, wout, gamma, beta, l3_w, l3_b, out):
    x1_dram = nc.dram_tensor("x1_dram", [NT, P, KC, TOK], F32, kind="Internal").ap()
    mod_dram = nc.dram_tensor("mod_dram", [NT, TAUS, TOK], F32, kind="Internal").ap()

    ctx = ExitStack()
    with ctx:
        base = (nc.sbuf_base + 63) // 64 * 64
        constants_at = [base + 202 * KIB]

        def place(name, kib, shape, dt=F32):
            return nc.alloc_sbuf_tensor_at(name, [P] + shape, dt, offset=base + int(kib * KIB))

        def const(name, n, dt=F32):
            at = constants_at[0]
            constants_at[0] += (4 * n + 31) // 32 * 32
            assert constants_at[0] <= nc.sbuf_usable_end
            return nc.alloc_sbuf_tensor_at(name, [P, n], dt, offset=at)

        def sem(name):
            return ctx.enter_context(nc.semaphore(name))

        NB = KC + SH + 1
        wa = place("wa", 0, [HC, 2, NB, P], F32R)
        x_hl = [place(f"x_hl{s}", 128 + 16 * s, [2, KC, TOK], F32R) for s in range(2)]
        x_raw = [place(f"x_raw{s}", 160 + 8 * s, [KC, TOK]) for s in range(2)]
        h_raw = [place(f"h_raw{s}", 176 + 2 * s, [TOK]) for s in range(2)]
        h_hl = [place(f"h_hl{s}", 180 + 4 * s, [2, TOK], F32R) for s in range(3)]
        w_stage = [place(f"w_stage{s}", 192 + 4 * s, [NB, P]) for s in range(2)]
        e_stage = place("e_stage", 192, [HC, P])
        lx = place("lx", 0, [KC, DIM])
        wg_hl = place("wg_hl", 8, [2 * KC, 2, DIM], F32R)
        wsoma_hl = place("wsoma_hl", 40, [KC, 2, DIM], F32R)
        wtemp_hl = place("wtemp_hl", 56, [KC, 2, DIM], F32R)
        wout_hl = place("wout_hl", 72, [KC, 2, DIM], F32R)
        wn1_sb = place("wn1_sb", 88, [KC, P])
        soma = place("soma", 90, [KC, TOK])
        temporal = place("temporal", 98, [KC, TOK])
        x2_hl = place("x2_hl", 106, [2, KC, TOK], F32R)
        o_sb = place("o_sb", 106, [KC, TOK])
        pair = [place(f"pair{s}", 122 + 2 * s, [TOK]) for s in range(2)]
        gated = place("gated", 126, [TOK])
        xt = [place(f"xt{s}", 128 + 8 * s, [KC, TOK]) for s in range(3)]
        ctx_hl = place("ctx_hl", 152, [2, KC, TOK], F32R)
        ts_hl = place("ts_hl", 168, [2, KC, TOK], F32R)
        mod_t = place("mod_t", 184, [TAUS, TOK])
        drive = [place(f"drive{s}", 192 + 2 * s, [TOK]) for s in range(2)]
        sumsq = place("sumsq", 196, [TOK])
        rstd = place("rstd", 198, [TOK])
        h1 = place("h1", 200, [TOK])
        mod_row = place("mod_row", 200, [TOK])
        b_stage = [place(f"b_stage{s}", 192 + 4 * s, [2, DIM]) for s in range(2)]
        B_SPLIT = [(dram, hl, 2 * q) for dram, hl, n in ((wg, wg_hl, 2 * KC), (wsoma, wsoma_hl, KC),
                                                         (wtemp, wtemp_hl, KC), (wout, wout_hl, KC))
                   for q in range(n // 2)]
        NBS = len(B_SPLIT)
        FIRST_OUT = NBS - KC // 2
        idx = const("idx", 2 * B, I32)
        fc1_b_sb = const("fc1_b_sb", HC)
        fc2_b_sb = const("fc2_b_sb", SH)
        exp_b_sb = const("exp_b_sb", B)
        l1_b_sb = const("l1_b_sb", B * KC)
        l3_b_sb = const("l3_b_sb", B * KC)
        tau_sb = const("tau_sb", 1 + TAUS)
        alpha = const("alpha", 1 + TAUS)
        bg_sb = const("bg_sb", KC)
        bn1_sb = const("bn1_sb", 1)
        wn2_sb = const("wn2_sb", TAUS)
        bn2_sb = const("bn2_sb", 1)
        blend_sb = const("blend_sb", KC * TAUS)
        blend_max = const("blend_max", KC)
        bsoma_sb = const("bsoma_sb", KC)
        btemp_sb = const("btemp_sb", KC)
        gamma_sb = const("gamma_sb", KC)
        beta_sb = const("beta_sb", KC)
        wout_mean = const("wout_mean", 2)
        eps_sb = const("eps_sb", 1)
        ctx_last = const("ctx_last", KC)
        trace_last = const("trace_last", KC * TAUS)
        ones = const("ones", P)

        bank = [ctx.enter_context(nc.psum_tensor(f"bank{i}", [P, TOK], F32)) for i in range(8)]
        acc = bank[0:KC]
        fc1_ring = bank[KC:8]

        s_idx = sem("s_idx")
        s_small = sem("s_small")
        s_wst = [sem(f"s_wst{s}") for s in range(2)]
        s_whi = sem("s_whi")
        s_wlo = sem("s_wlo")
        s_est = sem("s_est")
        s_ehi = sem("s_ehi")
        s_elo = sem("s_elo")
        s_xld = [sem(f"s_xld{s}") for s in range(2)]
        s_xhi = sem("s_xhi")
        s_xlo = sem("s_xlo")
        s_fc1 = sem("s_fc1")
        s_gelu = sem("s_gelu")
        s_hhi = sem("s_hhi")
        s_hlo = sem("s_hlo")
        s_fc2 = sem("s_fc2")
        s_x1 = sem("s_x1")
        s_x1st = sem("s_x1st")
        s_bst = [sem(f"s_bst{s}") for s in range(2)]
        s_cen = sem("s_cen")
        s_bhi = sem("s_bhi")
        s_blo = sem("s_blo")
        s_n1w = sem("s_n1w")
        s_lx = sem("s_lx")
        s_xt = [sem(f"s_xt{s}") for s in range(3)]
        s_cst = sem("s_cst")
        s_blend_c = sem("s_blend_c")
        s_exp = sem("s_exp")
        s_pe = {k: sem("s_pe_" + k) for k in
                ("L1", "N1", "SO", "MO", "WG", "TE", "OU", "SS", "L3")}
        s_x2 = sem("s_x2")
        s_x2hi = sem("s_x2hi")
        s_x2lo = sem("s_x2lo")
        s_ctx = sem("s_ctx")
        s_ctxl = sem("s_ctxl")
        s_ctxhi = sem("s_ctxhi")
        s_ctxlo = sem("s_ctxlo")
        s_h1 = sem("s_h1")
        s_soma = sem("s_soma")
        s_mod = sem("s_mod")
        s_mst = sem("s_mst")
        s_mld = sem("s_mld")
        s_wgt = sem("s_wgt")
        s_gated = sem("s_gated")
        s_drive = sem("s_drive")
        s_trace = sem("s_trace")
        s_tracel = sem("s_tracel")
        s_blend = sem("s_blend")
        s_temphi = sem("s_temphi")
        s_templo = sem("s_templo")
        s_gate = sem("s_gate")
        s_spk = sem("s_spk")
        s_spkhi = sem("s_spkhi")
        s_spklo = sem("s_spklo")
        s_o = sem("s_o")
        s_sq = sem("s_sq")
        s_ssq = sem("s_ssq")
        s_std = sem("s_std")
        s_rstd = sem("s_rstd")
        s_z = sem("s_z")
        s_x3 = sem("s_x3")
        s_y = sem("s_y")
        s_out = sem("s_out")

        SMALL = [(fc1_b_sb, fc1_b), (tau_sb, taus), (blend_sb, blend), (fc2_b_sb, fc2_b), (bg_sb, bg),
                 (bn1_sb, bn1), (wn2_sb, wn2), (bn2_sb, bn2), (bsoma_sb, bsoma), (btemp_sb, btemp),
                 (gamma_sb, gamma), (beta_sb, beta)]
        N_SMALL = 16 * (len(SMALL) + 3 * B)

        class Waits:

            def __init__(self, eng):
                self.eng, self.seen = eng, {}

            def __call__(self, s, value):
                if value > self.seen.get(s.name, 0):
                    self.seen[s.name] = value
                    self.eng.wait_ge(s, value)

        CHUNKS = dict(L1=KC, N1=1, SO=KC, MO=1, WG=KC, TE=KC, OU=KC, SS=1, L3=KC)
        LAG = dict(L1=0, SS=2, N1=0, SO=0, L3=2, MO=0, WG=0, TE=1, OU=1)
        READ = dict(L1=s_x2, N1=s_h1, SO=s_soma, MO=s_mod, WG=s_gated, TE=s_spk, OU=s_ssq, SS=s_rstd, L3=s_y)

        def rounds(steps):
            return [(k, r - lag, m) for r in range(NT + 2) for k, lag, m in steps if 0 <= r - lag < NT]

        def chunks(k, ms=None):
            return [(k, LAG[k], m) for m in (range(CHUNKS[k]) if ms is None else ms)]

        PE_ORDER = rounds(chunks("L1", (0, 1)) + chunks("SS") + chunks("L1", (2, 3)) + chunks("TE") +
                          chunks("N1") + chunks("MO") + chunks("WG") + chunks("L3") + chunks("SO") +
                          chunks("OU"))
        ACT_ORDER = rounds([("SS", 2, 0)] + [("X2H", 0, c) for c in range(KC)] +
                           [("TE", 1, 0), ("TE", 1, 1), ("CTXH", 0, 0), ("CTXH", 0, 1), ("TE", 1, 2),
                            ("CTXH", 0, 2), ("TE", 1, 3), ("CTXH", 0, 3), ("N1", 0, 0), ("MO", 0, 0)] +
                           [("SPKH", 1, c) for c in range(KC)] + chunks("WG") + chunks("SO") +
                           chunks("OU") + [("TEMPH", 0, c) for c in range(KC)])
        V_ORDER = rounds([("SS", 2, 0), ("L1", 0, 0), ("CTX", 0, 0), ("TE", 1, 0), ("WG", 0, 0), ("WG", 0, 1),
                          ("WG", 0, 2), ("L3", 2, 0), ("WG", 0, 3), ("OU", 1, 0), ("TEMPL", 0, 0)])
        bank_of = {key: bank[n % 8] for n, key in enumerate(PE_ORDER)}
        before = {key: PE_ORDER[n - 8] if n >= 8 else None for n, key in enumerate(PE_ORDER)}
        LX_LOADS, lx_load_of = [], {}
        last_use = None
        for k, i, m in PE_ORDER:
            if k in ("L1", "L3") and (k, i) not in lx_load_of:
                if not LX_LOADS or LX_LOADS[-1][0:2] != (k, i // HALVES):
                    LX_LOADS.append((k, i // HALVES, last_use))
                lx_load_of[k, i] = len(LX_LOADS)
                last_use = (k, i)
        last_fc2 = NT * HC

        block = ctx.enter_context(nc.Block())

        @block.sync
        def _(eng):
            wait = Waits(eng)
            eng.dma_start(idx[0:1, 0:B], tok16).then_inc(s_idx, 16)
            eng.dma_start(idx[0:1, B:2 * B], tok8).then_inc(s_idx, 16)
            eng.dma_start(x_raw[0][:, :, :], x[0]).then_inc(s_xld[0], 16)
            wait(s_idx, 32)
            expert = [nc.sync.value_load(idx[0:1, b:b + 1], min_val=0, max_val=EXPERTS - 1) for b in range(B)]
            subject = [nc.sync.value_load(idx[0:1, B + b:B + b + 1], min_val=0, max_val=SUBJECTS - 1)
                       for b in range(B)]

            def load_weights(j):
                if j >= 2:
                    wait(s_wlo, j - 1)
                st = w_stage[j % 2]
                eng.dma_start(st[:, 0:KC, :], fc1_w[j]).then_inc(s_wst[j % 2], 16)
                eng.dma_start(st[:, KC:KC + SH, :], fc2_w[j]).then_inc(s_wst[j % 2], 16)
                eng.dma_start(st[:, NB - 1:NB, :],
                              exp_w[bass.ds(expert[0], 1), :, j:j + 1, :].rearrange("e p a n -> p (e a) n")
                              ).then_inc(s_wst[j % 2], 16)

            load_weights(0)
            load_weights(1)
            for j in range(2, HC):
                load_weights(j)
                if j == 4:
                    eng.dma_start(x_raw[1][:, :, :], x[1]).then_inc(s_xld[1], 16)
            for t in range(NT - 1):
                b = t // HALVES
                if t % HALVES == 0 and b + 1 < B:
                    wait(s_wlo, HC)
                    wait(s_elo, HC * b)
                    eng.dma_start(e_stage[:, :, :],
                                  exp_w[bass.ds(expert[b + 1], 1), :, :, :].rearrange("e p a n -> p (e a) n")
                                  ).then_inc(s_est, 16)
                wait(s_x1, KC * (t + 1))
                eng.dma_start(x1_dram[t], x_raw[t % 2][:, :, :]).then_inc(s_x1st, 16)
                if t + 2 < NT:
                    wait(s_x1st, 16 * (t + 1))
                    eng.dma_start(x_raw[t % 2][:, :, :], x[t + 2]).then_inc(s_xld[t % 2], 16)

            def chunk_left(j):
                wait(s_fc2, (NT - 1) * HC + j + 1)

            def load_lx(n):
                k, b, use = LX_LOADS[n]
                if use:
                    wait(s_pe[use[0]], KC * (use[1] + 1))
                src = l1_w[bass.ds(subject[b], 1), :, :, :] if k == "L1" else \
                    l3_w[bass.ds(expert[b], 1), :, :, :]
                eng.dma_start(lx[:, :, :], src.rearrange("e p c n -> p (e c) n")).then_inc(s_lx, 16)

            def load_stage(q):
                dram, _, c = B_SPLIT[q]
                if q >= 2:
                    wait(s_blo, q - 1)
                eng.dma_start(b_stage[q % 2][:, :, :], dram[:, c:c + 2, :]).then_inc(s_bst[q % 2], 16)

            def load_xt(i):
                eng.dma_start(xt[i % 3][:, :, :], x1_dram[i]).then_inc(s_xt[i % 3], 16)

            wait(s_elo, HC * (B - 1))
            load_stage(0)
            load_stage(1)
            wait(s_x1st, 16 * 2)
            wait(s_fc1, (NT - 1) * HC)
            load_xt(0)
            load_xt(1)
            chunk_left(0)
            load_lx(0)
            for q in range(2, NBS):
                load_stage(q)
            chunk_left(11)
            eng.dma_start(wn1_sb[:, :, :], wn1).then_inc(s_n1w, 16)
            wait(s_x1, KC * NT)
            eng.dma_start(x1_dram[NT - 1], x_raw[(NT - 1) % 2][:, :, :]).then_inc(s_x1st, 16)
            wait(s_x1st, 16 * NT)
            wait(s_fc2, last_fc2)
            load_xt(2)
            loads = 1
            for r in range(NT + 2):
                while loads < len(LX_LOADS) and LX_LOADS[loads][2][1] + LAG[LX_LOADS[loads][2][0]] <= r:
                    load_lx(loads)
                    loads += 1
                i = r - LAG["L3"]
                if i >= 0:
                    wait(s_y, KC * (i + 1))
                    eng.dma_start(out[i], xt[i % 3][:, :, :]).then_inc(s_out, 16)
                    if i + 3 < NT:
                        wait(s_out, 16 * (i + 1))
                        load_xt(i + 3)
            wait(s_out, 16 * NT)

        @block.gpsimd
        def _(eng):
            wait = Waits(eng)
            for dst, src in SMALL:
                eng.dma_start(dst[0:src.shape[0], :], src).then_inc(s_small, 16)
            wait(s_idx, 32)
            expert = [nc.gpsimd.value_load(idx[0:1, b:b + 1], min_val=0, max_val=EXPERTS - 1) for b in range(B)]
            subject = [nc.gpsimd.value_load(idx[0:1, B + b:B + b + 1], min_val=0, max_val=SUBJECTS - 1)
                       for b in range(B)]
            for b in range(B):
                eng.dma_start(exp_b_sb[:, b:b + 1], exp_b[bass.ds(expert[b], 1), :].rearrange("e p -> p e")
                              ).then_inc(s_small, 16)
                eng.dma_start(l1_b_sb[:, b * KC:(b + 1) * KC],
                              l1_b[bass.ds(subject[b], 1), :, :].rearrange("e p c -> p (e c)")
                              ).then_inc(s_small, 16)
                eng.dma_start(l3_b_sb[:, b * KC:(b + 1) * KC],
                              l3_b[bass.ds(expert[b], 1), :, :].rearrange("e p c -> p (e c)")
                              ).then_inc(s_small, 16)
            for i in range(NT):
                wait(s_mod, i + 1)
                eng.dma_start(mod_dram[i], mod_row[0:TAUS, :]).then_inc(s_mst, 16)
                wait(s_mst, 16 * (i + 1))
                if i:
                    wait(s_drive, KC * TAUS * i)
                eng.dma_start(mod_t[:, :, :], mod_dram[i:i + 1, :, :].to_broadcast([P, TAUS, TOK])
                              ).then_inc(s_mld, 16)

        @block.scalar
        def _(eng):
            wait = Waits(eng)
            def w_hi(j):
                wait(s_wst[j % 2], 48 * (j // 2 + 1))
                eng.activation(wa[:, j, 0, :, :], w_stage[j % 2][:, :, :], ACT.Copy).then_inc(s_whi, 1)

            def x_hi(t, c):
                wait(s_xld[t % 2], 16 * (t // 2 + 1))
                if t >= 2:
                    wait(s_fc1, HC * (t - 1))
                eng.activation(x_hl[t % 2][:, 0, c, :], x_raw[t % 2][:, c, :], ACT.Copy).then_inc(s_xhi, 1)

            for c in range(KC):
                x_hi(0, c)
            w_hi(0)
            w_hi(1)
            wait(s_small, N_SMALL)
            eng.activation(alpha[:, :], tau_sb[:, :], ACT.Exp).then_inc(s_exp, 1)
            wait(s_cst, 2)
            eng.activation(blend_sb[:, :], blend_sb[:, :], ACT.Exp).then_inc(s_exp, 1)
            for u in range(NT * HC):
                t, j = divmod(u, HC)
                if t == 0 and j + 2 < HC:
                    w_hi(j + 2)
                wait(s_fc1, u + 1)
                if u >= 2:
                    wait(s_hlo, u - 1)
                eng.activation(h_raw[u % 2][:, :], fc1_ring[u % 4][:, :], ACT.Gelu,
                               bias=fc1_b_sb[:, j:j + 1]).then_inc(s_gelu, 1)
                wait(s_gelu, u + 1)
                if u >= 3:
                    wait(s_fc2, u - 2)
                eng.activation(h_hl[u % 3][:, 0, :], h_raw[u % 2][:, :], ACT.Copy).then_inc(s_hhi, 1)
                if 4 <= j < 4 + KC and t + 1 < NT:
                    x_hi(t + 1, j - 4)
                v = u - 4
                if v >= 0 and (v // HC) % HALVES == HALVES - 1 and v // HC < NT - 1:
                    b, je = v // HC // HALVES, v % HC
                    wait(s_est, 16 * (b + 1))
                    wait(s_fc2, v + 1)
                    eng.activation(wa[:, je, 0, NB - 1, :], e_stage[:, je, :], ACT.Copy).then_inc(s_ehi, 1)
                q = v - (NT - 1) * HC - 1
                if 0 <= q < NBS:
                    _, hl, c = B_SPLIT[q]
                    wait(s_bst[q % 2], 16 * (q // 2 + 1))
                    if q >= FIRST_OUT:
                        wait(s_cen, 4 * (q - FIRST_OUT + 1))
                    wait(s_fc2, v + 1)
                    eng.activation(hl[:, c:c + 2, 0, :], b_stage[q % 2][:, :, :], ACT.Copy).then_inc(s_bhi, 1)

            for k, i, m in ACT_ORDER:
                n = CHUNKS.get(k, KC) * i + m
                if k in CHUNKS:
                    ps = bank_of[k, i, m]
                    wait(s_pe[k], n + 1)
                if k == "SS":
                    eng.activation(ps[:, :], ps[:, :], ACT.Sqrt, bias=eps_sb[:, 0:1],
                                   scale=1.0 / DIM).then_inc(s_std, 1)
                elif k == "X2H":
                    wait(s_x2, n + 1)
                    if i:
                        wait(s_pe["SO"], KC * i)
                    if i >= 2:
                        wait(s_z, KC * (i - 1))
                    eng.activation(x2_hl[:, 0, m, :], xt[i % 3][:, m, :], ACT.Copy).then_inc(s_x2hi, 1)
                elif k == "CTXH":
                    wait(s_x1st, 16 * NT)
                    wait(s_ctx, n + 1)
                    if i:
                        wait(s_pe["WG"], KC * i)
                    eng.activation(ctx_hl[:, 0, m, :], pair[m % 2][:, :], ACT.Copy).then_inc(s_ctxhi, 1)
                elif k == "N1":
                    if i:
                        wait(s_mst, 16 * i)
                    eng.activation(h1[:, :], ps[:, :], ACT.Gelu, bias=bn1_sb[:, 0:1]).then_inc(s_h1, 1)
                elif k == "MO":
                    eng.activation(mod_row[0:TAUS, :], ps[0:TAUS, :], ACT.Tanh, bias=bn2_sb[0:TAUS, 0:1],
                                   scale=0.5).then_inc(s_mod, 1)
                elif k == "WG":
                    eng.activation(ps[:, :], ps[:, :], ACT.Tanh, bias=bg_sb[:, m:m + 1],
                                   scale=0.5).then_inc(s_wgt, 1)
                elif k == "TEMPH":
                    wait(s_blend, TAUS * (n + 1))
                    if i:
                        wait(s_pe["OU"], KC * i)
                    eng.activation(ts_hl[:, 0, m, :], temporal[:, m, :], ACT.Copy).then_inc(s_temphi, 1)
                elif k == "TE":
                    eng.activation(ps[:, :], ps[:, :], ACT.Tanh, bias=btemp_sb[:, m:m + 1],
                                   scale=0.5).then_inc(s_gate, 1)
                elif k == "SPKH":
                    wait(s_spk, n + 1)
                    wait(s_pe["TE"], KC * (i + 1))
                    eng.activation(ts_hl[:, 0, m, :], pair[m % 2][:, :], ACT.Copy).then_inc(s_spkhi, 1)
                elif k == "SO":
                    if i:
                        wait(s_spk, KC * (i - 1) + m + 1)
                    eng.activation(soma[:, m, :], ps[:, :], ACT.Gelu,
                                   bias=bsoma_sb[:, m:m + 1]).then_inc(s_soma, 1)
                elif k == "OU":
                    if i + 1 < NT:
                        wait(s_pe["SO"], KC * (i + 2))
                    else:
                        wait(s_pe["SO"], KC * NT)
                    eng.activation(o_sb[:, m, :], ps[:, :], ACT.Copy).then_inc(s_o, 1)
                    wait(s_o, n + 1)
                    eng.activation(ps[:, :], ps[:, :], ACT.Square).then_inc(s_sq, 1)

        @block.tensor
        def _(eng):
            wait = Waits(eng)

            def split_product(ps, w_hi, w_lo, x_hi, x_lo, first, last):
                eng.matmul(ps, w_hi, x_hi, start=first, stop=False)
                eng.matmul(ps, w_hi, x_lo, start=False, stop=False)
                return eng.matmul(ps, w_lo, x_hi, start=False, stop=last)

            def fc1(u):
                t, j = divmod(u, HC)
                wait(s_wlo, j + 1)
                wait(s_xlo, KC * (t + 1))
                if u >= 4:
                    wait(s_gelu, u - 3)
                for c in range(KC):
                    mm = split_product(fc1_ring[u % 4][:, :], wa[:, j, 0, c, :], wa[:, j, 1, c, :],
                                       x_hl[t % 2][:, 0, c, :], x_hl[t % 2][:, 1, c, :], c == 0, c == KC - 1)
                mm.then_inc(s_fc1, 1)

            def fc2(u):
                t, j = divmod(u, HC)
                wait(s_hlo, u + 1)
                b = t // HALVES
                if b:
                    wait(s_elo, HC * (b - 1) + j + 1)
                if j == 0 and t:
                    wait(s_x1, KC * t)
                for m in range(KC):
                    mm = split_product(acc[m][:, :], wa[:, j, 0, KC + m, :], wa[:, j, 1, KC + m, :],
                                       h_hl[u % 3][:, 0, :], h_hl[u % 3][:, 1, :], j == 0, j == HC - 1)
                mm.then_inc(s_fc2, 1)

            for u in range(NT * HC + 2):
                if u < NT * HC:
                    fc1(u)
                if u >= 2:
                    fc2(u - 2)

            wait(s_x1, KC * NT)
            wait(s_gelu, NT * HC)
            for k, i, m in PE_ORDER:
                ps = bank_of[k, i, m]
                if before[k, i, m]:
                    bk, bi, bm = before[k, i, m]
                    wait(READ[bk], CHUNKS[bk] * bi + bm + 1)
                cols = slice(m * P, (m + 1) * P)
                raw = [xt[i % 3][:, c, :] for c in range(KC)]
                if k in ("WG", "SO", "TE", "OU"):
                    w_hl = dict(WG=wg_hl, SO=wsoma_hl, TE=wtemp_hl, OU=wout_hl)[k]
                    n_in = 2 * KC if k == "WG" else KC
                    wait(s_blo, dict(WG=4, SO=6, TE=8, OU=NBS)[k])
                    if k == "TE":
                        wait(s_temphi, KC * (i + 1))
                        wait(s_templo, KC * (i + 1))
                    elif k == "OU":
                        wait(s_spkhi, KC * (i + 1))
                        wait(s_spklo, KC * (i + 1))
                    else:
                        wait(s_x2hi, KC * (i + 1))
                        wait(s_x2lo, KC * (i + 1))
                    for c in range(n_in):
                        if c == KC:
                            wait(s_ctxhi, KC * (i + 1))
                            wait(s_ctxlo, KC * (i + 1))
                        hl = ctx_hl if c >= KC else x2_hl if k in ("WG", "SO") else ts_hl
                        mm = split_product(ps[:, :], w_hl[:, c, 0, cols], w_hl[:, c, 1, cols],
                                           hl[:, 0, c % KC, :], hl[:, 1, c % KC, :], c == 0, c == n_in - 1)
                    mm.then_inc(s_pe[k], 1)
                    continue
                rows = slice(0, P)
                if k == "L1":
                    wait(s_lx, 16 * lx_load_of[k, i])
                    wait(s_xt[i % 3], 16 * (i // 3 + 1))
                    terms = [(lx[:, c, cols], raw[c]) for c in range(KC)]
                elif k == "N1":
                    wait(s_n1w, 16)
                    wait(s_x2, KC * (i + 1))
                    terms = [(wn1_sb[:, c, :], raw[c]) for c in range(KC)]
                elif k == "MO":
                    wait(s_h1, i + 1)
                    rows = slice(0, TAUS)
                    terms = [(wn2_sb[:, :], h1[:, :])]
                elif k == "SS":
                    wait(s_cst, 1)
                    wait(s_ssq, KC * (i + 1))
                    terms = [(ones[:, :], sumsq[:, :])]
                elif k == "L3":
                    wait(s_lx, 16 * lx_load_of[k, i])
                    wait(s_x3, KC * (i + 1))
                    terms = [(lx[:, c, cols], raw[c]) for c in range(KC)]
                for n, (w, r) in enumerate(terms):
                    mm = eng.matmul(ps[rows, :], w, r, start=n == 0, stop=n == len(terms) - 1)
                mm.then_inc(s_pe[k], 1)

        @block.vector
        def _(eng):
            wait = Waits(eng)

            def w_lo(j):
                wait(s_whi, j + 1)
                eng.tensor_tensor(wa[:, j, 1, :, :], w_stage[j % 2][:, :, :], wa[:, j, 0, :, :].bitcast(F32),
                                  ALU.subtract).then_inc(s_wlo, 1)

            def x_lo(t, c):
                wait(s_xhi, KC * t + c + 1)
                eng.tensor_tensor(x_hl[t % 2][:, 1, c, :], x_raw[t % 2][:, c, :],
                                  x_hl[t % 2][:, 0, c, :].bitcast(F32), ALU.subtract).then_inc(s_xlo, 1)

            for c in range(KC):
                x_lo(0, c)
            w_lo(0)
            w_lo(1)
            eng.memset(ones[:, :], 1.0)
            eng.memset(eps_sb[:, :], 1e-5).then_inc(s_cst, 1)
            wait(s_small, N_SMALL)
            eng.tensor_scalar(bg_sb[:, :], bg_sb[:, :], 0.5, None, ALU.mult)
            eng.tensor_scalar(bn2_sb[0:TAUS, :], bn2_sb[0:TAUS, :], 0.5, None, ALU.mult)
            eng.tensor_scalar(btemp_sb[:, :], btemp_sb[:, :], 0.5, None, ALU.mult)
            blend_v = blend_sb[:, :].rearrange("p (c d) -> p c d", d=TAUS)
            links = [0]

            def link(ins):
                links[0] += 1
                ins.then_inc(s_blend_c, 1)
                wait(s_blend_c, links[0])

            link(eng.tensor_reduce(blend_max[:, :], blend_v, AX.X, ALU.max))
            for c in range(KC):
                ins = eng.tensor_scalar(blend_v[:, c, :], blend_v[:, c, :], blend_max[:, c:c + 1], None,
                                        ALU.subtract)
            ins.then_inc(s_cst, 1)
            wait(s_exp, 2)
            link(eng.tensor_reduce(blend_max[:, :], blend_v, AX.X, ALU.add))
            link(eng.reciprocal(blend_max[:, :], blend_max[:, :]))
            for c in range(KC):
                eng.tensor_scalar(blend_v[:, c, :], blend_v[:, c, :], blend_max[:, c:c + 1], 0.25,
                                  ALU.mult, ALU.mult)
            link(eng.tensor_scalar(alpha[:, :], alpha[:, :], 1.0, None, ALU.add))
            link(eng.reciprocal(alpha[:, :], alpha[:, :]))

            for u in range(NT * HC + 2):
                t, j = divmod(u, HC)
                if t == 0 and j + 2 < HC:
                    w_lo(j + 2)
                if u < NT * HC:
                    wait(s_hhi, u + 1)
                    if u >= 3:
                        wait(s_fc2, u - 2)
                    eng.tensor_tensor(h_hl[u % 3][:, 1, :], h_raw[u % 2][:, :],
                                      h_hl[u % 3][:, 0, :].bitcast(F32), ALU.subtract).then_inc(s_hlo, 1)
                if t and j == 1:
                    wait(s_fc2, HC * t)
                    for m in range(KC):
                        eb = (t - 1) // HALVES
                        bias = fc2_b_sb[:, m:m + 1] if m < SH else exp_b_sb[:, eb:eb + 1]
                        xr = x_raw[(t - 1) % 2][:, m, :]
                        eng.scalar_tensor_tensor(xr, acc[m][:, :], bias, xr, ALU.add, ALU.add
                                                 ).then_inc(s_x1, 1)
                if 4 <= j < 4 + KC and t + 1 < NT:
                    x_lo(t + 1, j - 4)
                v = u - 4
                if v >= 0 and (v // HC) % HALVES == HALVES - 1 and v // HC < NT - 1:
                    b, je = v // HC // HALVES, v % HC
                    wait(s_ehi, HC * b + je + 1)
                    eng.tensor_tensor(wa[:, je, 1, NB - 1, :], e_stage[:, je, :],
                                      wa[:, je, 0, NB - 1, :].bitcast(F32), ALU.subtract).then_inc(s_elo, 1)
                q = v - (NT - 1) * HC - 1
                if 0 <= q < NBS:
                    _, hl, c = B_SPLIT[q]
                    st = b_stage[q % 2]
                    if q >= FIRST_OUT:
                        n = 4 * (q - FIRST_OUT)
                        wait(s_bst[q % 2], 16 * (q // 2 + 1))
                        eng.tensor_reduce(wout_mean[:, :], st[:, :, :], AX.X, ALU.add).then_inc(s_cen, 1)
                        wait(s_cen, n + 1)
                        eng.tensor_scalar(wout_mean[:, :], wout_mean[:, :], 1.0 / DIM, None, ALU.mult
                                          ).then_inc(s_cen, 1)
                        wait(s_cen, n + 2)
                        for a in range(2):
                            eng.tensor_scalar(st[:, a, :], st[:, a, :], wout_mean[:, a:a + 1], 0.5,
                                              ALU.subtract, ALU.mult).then_inc(s_cen, 1)
                        wait(s_cen, n + 4)
                    wait(s_bhi, q + 1)
                    eng.tensor_tensor(hl[:, c:c + 2, 1, :], st[:, :, :], hl[:, c:c + 2, 0, :].bitcast(F32),
                                      ALU.subtract).then_inc(s_blo, 1)

            for k, i, part in V_ORDER:
                b = i // HALVES
                xi = xt[i % 3]
                first_half = i % HALVES == 0
                if k == "SS":
                    wait(s_std, i + 1)
                    eng.reciprocal(rstd[:, :], bank_of[k, i, 0][:, :]).then_inc(s_rstd, 1)
                    wait(s_rstd, i + 1)
                    wait(s_o, KC * (i + 1))

                    def normal_of(m):
                        n = KC * i + m
                        if m < 2:
                            wait(s_spkhi, KC * (i + 1))
                            wait(s_spklo, KC * (i + 1))
                            if i + 1 < NT:
                                wait(s_ctxhi, KC * (i + 2))
                                wait(s_ctxlo, KC * (i + 2))
                        else:
                            wait(s_x3, n - 1)
                        eng.scalar_tensor_tensor(pair[m % 2][:, :], o_sb[:, m, :], gamma_sb[:, m:m + 1],
                                                 rstd[:, :], ALU.mult, ALU.mult).then_inc(s_z, 1)

                    def x3_of(m):
                        wait(s_z, KC * i + m + 1)
                        eng.scalar_tensor_tensor(xi[:, m, :], pair[m % 2][:, :], beta_sb[:, m:m + 1],
                                                 xi[:, m, :], ALU.add, ALU.add).then_inc(s_x3, 1)

                    normal_of(0)
                    for m in range(KC):
                        if m + 1 < KC:
                            normal_of(m + 1)
                        x3_of(m)
                elif k == "L1":
                    for m in range(KC):
                        wait(s_pe["L1"], KC * (i + 1))
                        eng.scalar_tensor_tensor(xi[:, m, :], bank_of[k, i, m][:, :],
                                                 l1_b_sb[:, b * KC + m:b * KC + m + 1], xi[:, m, :],
                                                 ALU.add, ALU.add).then_inc(s_x2, 1)
                    for m in range(KC):
                        wait(s_x2hi, KC * i + m + 1)
                        eng.tensor_tensor(x2_hl[:, 1, m, :], xi[:, m, :], x2_hl[:, 0, m, :].bitcast(F32),
                                          ALU.subtract).then_inc(s_x2lo, 1)
                elif k == "CTX":
                    def context_of(c):
                        n = KC * i + c
                        if c >= 2:
                            wait(s_ctxhi, n - 1)
                            wait(s_ctxlo, n - 1)
                        else:
                            if i >= 2:
                                wait(s_spkhi, KC * (i - 1))
                                wait(s_spklo, KC * (i - 1))
                                wait(s_x3, KC * (i - 1))
                            if i:
                                wait(s_ctxhi, KC * i)
                                wait(s_ctxlo, KC * i)
                        start = 0.0
                        if not first_half:
                            wait(s_ctxl, KC * (i // HALVES) + c + 1)
                            start = ctx_last[:, c:c + 1]
                        eng.tensor_tensor_scan(pair[c % 2][:, :], alpha[:, 0:1].to_broadcast([P, TOK]),
                                               xi[:, c, :], start, ALU.mult, ALU.add).then_inc(s_ctx, 1)

                    def context_lo(c):
                        n = KC * i + c
                        if first_half:
                            wait(s_ctx, n + 1)
                            eng.tensor_copy(ctx_last[:, c:c + 1], pair[c % 2][:, TOK - 1:TOK]).then_inc(s_ctxl, 1)
                        wait(s_x1st, 16 * NT)
                        wait(s_ctxhi, n + 1)
                        eng.tensor_tensor(ctx_hl[:, 1, c, :], pair[c % 2][:, :], ctx_hl[:, 0, c, :].bitcast(F32),
                                          ALU.subtract).then_inc(s_ctxlo, 1)

                    context_of(0)
                    for c in range(KC):
                        if c + 1 < KC:
                            context_of(c + 1)
                        context_lo(c)
                elif k == "TE":
                    def spikes_of(m):
                        n = KC * i + m
                        if m >= 2:
                            wait(s_spkhi, n - 1)
                            wait(s_spklo, n - 1)
                        else:
                            wait(s_ctxhi, KC * min(i + 2, NT))
                            wait(s_ctxlo, KC * min(i + 2, NT))
                            if i:
                                wait(s_x3, KC * i)
                        wait(s_gate, n + 1)
                        wait(s_soma, n + 1)
                        eng.scalar_tensor_tensor(pair[m % 2][:, :], bank_of[k, i, m][:, :], 1.0,
                                                 soma[:, m, :], ALU.add, ALU.mult).then_inc(s_spk, 1)

                    def spikes_lo(m):
                        wait(s_spkhi, KC * i + m + 1)
                        eng.tensor_tensor(ts_hl[:, 1, m, :], pair[m % 2][:, :], ts_hl[:, 0, m, :].bitcast(F32),
                                          ALU.subtract).then_inc(s_spklo, 1)

                    spikes_of(0)
                    for m in range(KC):
                        if m + 1 < KC:
                            spikes_of(m + 1)
                        spikes_lo(m)
                elif k == "WG":
                    c, n = part, KC * i + part
                    wait(s_wgt, n + 1)
                    if n:
                        wait(s_drive, TAUS * n)
                    eng.scalar_tensor_tensor(gated[:, :], bank_of[k, i, c][:, :], 1.0, xi[:, c, :],
                                             ALU.add, ALU.mult).then_inc(s_gated, 1)
                    wait(s_gated, n + 1)
                    wait(s_mld, 16 * (i + 1))

                    def drive_of(d):
                        q = TAUS * n + d
                        if q >= 2:
                            wait(s_blend, q - 1)
                        eng.scalar_tensor_tensor(drive[q % 2][:, :], mod_t[:, d, :], 2.0, gated[:, :],
                                                 ALU.add, ALU.mult).then_inc(s_drive, 1)

                    def trace_of(d):
                        q = TAUS * n + d
                        wait(s_drive, q + 1)
                        start = 0.0
                        if not first_half:
                            wait(s_tracel, TAUS * KC * (i // HALVES) + TAUS * c + d + 1)
                            start = trace_last[:, TAUS * c + d:TAUS * c + d + 1]
                        eng.tensor_tensor_scan(drive[q % 2][:, :], alpha[:, 1 + d:2 + d].to_broadcast([P, TOK]),
                                               drive[q % 2][:, :], start, ALU.mult, ALU.add
                                               ).then_inc(s_trace, 1)

                    def blend_of(d):
                        q = TAUS * n + d
                        wait(s_trace, q + 1)
                        tr, te = drive[q % 2], temporal[:, c, :]
                        if first_half:
                            eng.tensor_copy(trace_last[:, TAUS * c + d:TAUS * c + d + 1],
                                            tr[:, TOK - 1:TOK]).then_inc(s_tracel, 1)
                        w = blend_sb[:, TAUS * c + d:TAUS * c + d + 1]
                        if d == 0:
                            if i:
                                wait(s_temphi, KC * (i - 1) + c + 1)
                                wait(s_templo, KC * (i - 1) + c + 1)
                            eng.tensor_scalar(te, tr[:, :], w, None, ALU.mult).then_inc(s_blend, 1)
                        else:
                            wait(s_blend, q)
                            eng.scalar_tensor_tensor(te, tr[:, :], w, te, ALU.mult, ALU.add
                                                     ).then_inc(s_blend, 1)

                    drive_of(0)
                    drive_of(1)
                    trace_of(0)
                    for d in range(1, TAUS):
                        trace_of(d)
                        blend_of(d - 1)
                        if d + 1 < TAUS:
                            drive_of(d + 1)
                    blend_of(TAUS - 1)
                elif k == "OU":
                    for m in range(KC):
                        n = KC * i + m
                        wait(s_sq, n + 1)
                        if m == 0:
                            if i:
                                wait(s_pe["SS"], i)
                            eng.tensor_copy(sumsq[:, :], bank_of[k, i, m][:, :]).then_inc(s_ssq, 1)
                        else:
                            wait(s_ssq, n)
                            eng.tensor_tensor(sumsq[:, :], bank_of[k, i, m][:, :], sumsq[:, :], ALU.add
                                              ).then_inc(s_ssq, 1)
                elif k == "TEMPL":
                    for c in range(KC):
                        wait(s_temphi, KC * i + c + 1)
                        eng.tensor_tensor(ts_hl[:, 1, c, :], temporal[:, c, :], ts_hl[:, 0, c, :].bitcast(F32),
                                          ALU.subtract).then_inc(s_templo, 1)
                elif k == "L3":
                    for m in range(KC):
                        wait(s_pe["L3"], KC * (i + 1))
                        eng.scalar_tensor_tensor(xi[:, m, :], bank_of[k, i, m][:, :],
                                                 l3_b_sb[:, b * KC + m:b * KC + m + 1], xi[:, m, :],
                                                 ALU.add, ALU.add).then_inc(s_y, 1)


def kernel(x, itok_B_0_15, itok_B_0_7, condB_tauraws, cond_256, condB_bn2, cond_1024, L0_cond_fc1_w,
           L0_cond_fc1_b, L0_cond_fc2_w, L0_cond_fc2_b, L0_cond_experts_w, L0_cond_experts_b,
           L1_cond_weight, L1_cond_bias, L2_cond_tau_ctx, L2_cond_Wg, L2_cond_bg, L2_cond_Wn1,
           L2_cond_bn1, L2_cond_Wsoma, L2_cond_bsoma, L2_cond_Wtemp, L2_cond_btemp, L2_cond_Wout,
           L2_cond_gamma, L2_cond_beta, L3_cond_weight, L3_cond_bias):
    import concourse.bacc as bacc
    from concourse.bass_utils import run_bass_kernel_spmd

    def a(v):
        return np.asarray(v)

    def stationary(w):
        o, i = w.shape
        return w.T.reshape(i // P, P, o).transpose(1, 0, 2)

    def columns(v):
        return v.reshape(-1, P).T

    data = {
        "x": a(x).reshape(B, HALVES, TOK, KC, P).transpose(0, 1, 4, 3, 2).reshape(NT, P, KC, TOK),
        "tok16": a(itok_B_0_15).reshape(1, B),
        "tok8": a(itok_B_0_7).reshape(1, B),
        "fc1_w": a(L0_cond_fc1_w).reshape(HC, P, KC, P).transpose(0, 3, 2, 1),
        "fc2_w": a(L0_cond_fc2_w).T.reshape(HC, P, SH, P),
        "exp_w": a(L0_cond_experts_w).reshape(EXPERTS, P, HC, P).transpose(0, 3, 2, 1),
        "fc1_b": columns(a(L0_cond_fc1_b)),
        "fc2_b": columns(a(L0_cond_fc2_b)),
        "exp_b": a(L0_cond_experts_b),
        "l1_w": a(L1_cond_weight).transpose(0, 2, 1).reshape(SUBJECTS, KC, P, DIM).transpose(0, 2, 1, 3),
        "l1_b": a(L1_cond_bias).reshape(SUBJECTS, KC, P).transpose(0, 2, 1),
        "taus": np.broadcast_to(np.concatenate([a(L2_cond_tau_ctx).reshape(1), a(condB_tauraws)]), (P, 1 + TAUS)),
        "wg": stationary(a(L2_cond_Wg)),
        "bg": columns(a(L2_cond_bg)),
        "wn1": stationary(a(L2_cond_Wn1)),
        "bn1": columns(a(L2_cond_bn1)),
        "wn2": a(cond_256).T,
        "bn2": a(condB_bn2).reshape(TAUS, 1),
        "blend": a(cond_1024).reshape(TAUS, KC, P).transpose(2, 1, 0).reshape(P, KC * TAUS),
        "wsoma": stationary(a(L2_cond_Wsoma)),
        "bsoma": columns(a(L2_cond_bsoma)),
        "wtemp": stationary(a(L2_cond_Wtemp)),
        "btemp": columns(a(L2_cond_btemp)),
        "wout": stationary(a(L2_cond_Wout)),
        "gamma": columns(a(L2_cond_gamma)),
        "beta": columns(a(L2_cond_beta)),
        "l3_w": a(L3_cond_weight).reshape(EXPERTS, KC, P, DIM).transpose(0, 2, 1, 3),
        "l3_b": a(L3_cond_bias).reshape(EXPERTS, KC, P).transpose(0, 2, 1),
    }
    nc = bacc.Bacc("TRN2", target_bir_lowering=False, num_devices=1)
    arrays, args = {}, []
    for name, v in data.items():
        arrays["in_" + name] = np.ascontiguousarray(v)
        args.append(nc.dram_tensor("in_" + name, v.shape, mybir.dt.from_np(v.dtype), kind="ExternalInput").ap())
    args.append(nc.dram_tensor("out", [NT, P, KC, TOK], F32, kind="ExternalOutput").ap())
    build(nc, *args)
    r = run_bass_kernel_spmd(nc, [arrays], core_ids=[0])
    y = r.results[0]["out"]
    return y.reshape(B, HALVES, P, KC, TOK).transpose(0, 1, 4, 3, 2).reshape(B, SEQ, DIM)
```

```python
import numpy as np
import concourse.bass as bass
from concourse import mybir
from contextlib import ExitStack

F32 = mybir.dt.float32
F32R = mybir.dt.float32r
I32 = mybir.dt.int32
ALU = mybir.AluOpType
ACT = mybir.ActivationFunctionType
AX = mybir.AxisListType

P = 128
B, SEQ, DIM = 4, 1024, 512
HID, EXPERTS, SUBJECTS = 2048, 16, 8
TAUS = 4
TOK = 512
HALVES = SEQ // TOK
NT = B * HALVES
KC = DIM // P
HC = HID // P
SH = KC - 1
KIB = 1024


SMALL = dict(fc1_b=HC, fc2_b=KC - 1, taus=1 + TAUS, blend=KC * TAUS, wn2=TAUS, bn1=1, bn2=1, bg=KC, bsoma=KC,
             btemp=KC, gamma=KC, beta=KC)


def build(nc, x, tok16, tok8, small, fc1_w, fc2_w, exp_w, exp_b, l1_w, l1_b, wg, wn1, wsoma, wtemp, wout,
          l3_w, l3_b, out):
    x2_dram = nc.dram_tensor("x2_dram", [NT, P, KC, TOK], F32, kind="Internal").ap()
    mod_dram = nc.dram_tensor("mod_dram", [NT, TAUS, TOK], F32, kind="Internal").ap()

    ctx = ExitStack()
    with ctx:
        base = (nc.sbuf_base + 63) // 64 * 64
        constants_at = [base + 204 * KIB]

        def place(name, kib, shape, dt=F32):
            return nc.alloc_sbuf_tensor_at(name, [P] + shape, dt, offset=base + int(kib * KIB))

        def const(name, n, dt=F32):
            at = constants_at[0]
            constants_at[0] += (4 * n + 31) // 32 * 32
            assert constants_at[0] <= nc.sbuf_usable_end
            return nc.alloc_sbuf_tensor_at(name, [P, n], dt, offset=at)

        def sem(name):
            return ctx.enter_context(nc.semaphore(name))

        NB = KC + SH + 1
        CHUNK_KIB = 2 * NB * P * 4 // KIB
        wa = place("wa", 0, [HC, 2, NB, P], F32R)
        x_hl = [place(f"x_hl{s}", 128 + 16 * s, [2, KC, TOK], F32R) for s in range(2)]
        x_raw = [place(f"x_raw{s}", 160 + 8 * s, [KC, TOK]) for s in range(2)]
        h_hl = [place(f"h_hl{s}", 176 + 4 * s, [2, TOK], F32R) for s in range(2)]
        l1_hl = place("l1_hl", 184, [KC, 2, DIM], F32R)
        stage = [place(f"stage{s}", 200 + 2 * s, [TOK]) for s in range(2)]
        EARLY = 8
        stage_early = [place(f"stage_early{s}", 184 + 2 * s, [TOK]) for s in range(EARLY)]
        l3w_hl = place("l3w_hl", 0, [KC, 2, DIM], F32R)
        l3w_raw = place("l3w_raw", 0, [KC, 2, DIM])
        x2_hl = place("x2_hl", 16, [2, KC, TOK], F32R)
        wg_hl = place("wg_hl", 32, [2 * KC, 2, DIM], F32R)
        wn1_hl = place("wn1_hl", 64, [2, KC, P], F32R)
        h1 = place("h1", 68, [TOK])
        mod_row = place("mod_row", 68, [TOK])
        gated = place("gated", 70, [TOK])
        mod_t = place("mod_t", 72, [TAUS, TOK])
        temporal = place("temporal", 80, [KC, TOK])
        temporal_lo = place("temporal_lo", 80, [KC, TOK], F32R)
        drive = [place(f"drive{s}", 88 + 2 * s, [TOK]) for s in range(2)]
        wsoma_hl = place("wsoma_hl", 96, [KC, 2, DIM], F32R)
        wout_hl = place("wout_hl", 112, [KC, 2, DIM], F32R)
        ctx_hi = place("ctx_hi", 128, [KC, TOK], F32R)
        ctx_raw = place("ctx_raw", 136, [KC, TOK])
        ctx_lo = place("ctx_lo", 136, [KC, TOK], F32R)
        o_sb = place("o_sb", 128, [KC, TOK])
        xt = [place(f"xt{s}", at, [KC, TOK]) for s, at in enumerate((160, 144, 176))]
        soma = place("soma", 152, [KC, TOK])
        spikes_lo = place("spikes_lo", 152, [KC, TOK], F32R)
        ts_hi = place("ts_hi", 168, [KC, TOK], F32R)
        wtemp_hl = place("wtemp_hl", 184, [KC, 2, DIM], F32R)
        sumsq = place("sumsq", 200, [TOK])
        diag = place("diag", 202, [TOK // P, P])
        x3_hi, x3_lo = [[place(f"x3_{part}{c}", at, [TOK], F32R) for c, at in enumerate(places)]
                        for part, places in (("hi", (136, 140, 92, 202)), ("lo", (138, 142, 94, 68)))]
        idx = const("idx", 2 * B, I32)
        small_sb = const("small_sb", sum(SMALL.values()))
        at = dict(zip(SMALL, np.cumsum([0] + list(SMALL.values())).tolist()))
        (fc1_b_sb, fc2_b_sb, tau_sb, blend_sb, wn2_sb, bn1_sb, bn2_sb, bg_sb, bsoma_sb, btemp_sb, gamma_sb,
         beta_sb) = [small_sb[:, at[k]:at[k] + n] for k, n in SMALL.items()]
        exp_b_sb = const("exp_b_sb", B)
        l1_b_sb = const("l1_b_sb", B * KC)
        l3_b_sb = const("l3_b_sb", B * KC)
        alpha = const("alpha", 1 + TAUS)
        blend_max = const("blend_max", KC)
        wout_mean = const("wout_mean", 1)
        eps_sb = const("eps_sb", 1)
        ctx_last = const("ctx_last", KC)
        trace_last = const("trace_last", KC * TAUS)
        std = const("std", TOK // P)
        rstd = const("rstd", TOK // P)
        ones = const("ones", P)
        ident = const("ident", P)

        bank = [ctx.enter_context(nc.psum_tensor(f"bank{i}", [P, TOK], F32)) for i in range(8)]
        acc = bank[0:KC]
        RING_A = bank[KC:8]

        s_idx = sem("s_idx")
        s_small = sem("s_small")
        s_pick = sem("s_pick")
        s_st = [sem(f"s_st{s}") for s in range(2)]
        s_early = [sem(f"s_early{s}") for s in range(EARLY)]
        s_sthi = sem("s_sthi")
        s_stlo = sem("s_stlo")
        s_cen = sem("s_cen")
        s_xld = [sem(f"s_xld{s}") for s in range(2)]
        s_x0 = [sem(f"s_x0{c}") for c in range(KC)]
        s_xhi = sem("s_xhi")
        s_xlo = sem("s_xlo")
        s_fc1 = sem("s_fc1")
        s_gelu = sem("s_gelu")
        s_hhi = sem("s_hhi")
        s_hlo = sem("s_hlo")
        s_fc2 = sem("s_fc2")
        s_x1 = sem("s_x1")
        s_x1hi = sem("s_x1hi")
        s_x1lo = sem("s_x1lo")
        s_x2 = sem("s_x2")
        s_x2st = sem("s_x2st")
        s_xt = [[sem(f"s_xt{s}{c}") for c in range(KC)] for s in range(3)]
        s_l3w = sem("s_l3w")
        s_w3hi = sem("s_w3hi")
        s_w3lo = sem("s_w3lo")
        s_cst = sem("s_cst")
        s_chain = sem("s_chain")
        s_exp = sem("s_exp")
        s_id = sem("s_id")
        s_pe = {k: sem("s_pe_" + k) for k in
                ("L1", "N1", "SO", "MO", "WG", "TE", "OU", "SS", "RB", "L3")}
        s_x2free = sem("s_x2free")
        s_x2hi = sem("s_x2hi")
        s_x2lo = sem("s_x2lo")
        s_ctx = sem("s_ctx")
        s_ctxl = sem("s_ctxl")
        s_ctxhi = sem("s_ctxhi")
        s_ctxlo = sem("s_ctxlo")
        s_h1 = sem("s_h1")
        s_soma = sem("s_soma")
        s_mod = sem("s_mod")
        s_mst = sem("s_mst")
        s_mld = sem("s_mld")
        s_wgt = sem("s_wgt")
        s_gated = sem("s_gated")
        s_drive = sem("s_drive")
        s_trace = sem("s_trace")
        s_tracel = sem("s_tracel")
        s_blend0 = sem("s_blend0")
        s_blend = sem("s_blend")
        s_temphi = sem("s_temphi")
        s_templo = sem("s_templo")
        s_gate = sem("s_gate")
        s_spk = sem("s_spk")
        s_spkhi = sem("s_spkhi")
        s_spklo = sem("s_spklo")
        s_o = sem("s_o")
        s_sq = sem("s_sq")
        s_ssq = sem("s_ssq")
        s_std = sem("s_std")
        s_rstd = sem("s_rstd")
        s_diag = sem("s_diag")
        s_z = sem("s_z")
        s_x3 = sem("s_x3")
        s_x3hi = sem("s_x3hi")
        s_x3lo = sem("s_x3lo")
        s_y = sem("s_y")
        s_out = [sem(f"s_out{c}") for c in range(KC)]

        class Waits:

            def __init__(self, eng):
                self.eng, self.seen = eng, {}

            def __call__(self, s, value):
                if value > self.seen.get(s.name, 0):
                    self.seen[s.name] = value
                    self.eng.wait_ge(s, value)

        UNITS = NT * HC
        CONST_UNIT = HC + 10
        L1_UNIT = 5
        SPLIT_UNIT = HC - KC - 1

        STAGES = []

        def stage_weights(parts, hi, lo, unit, free=None, center=False):
            STAGES.append((parts, hi, lo, unit, free, center))
            return len(STAGES)

        def blocks(n):
            return lambda st: st[:, :].rearrange("p (c n) -> p c n", n=P)[:, n[0]:n[1], :]

        def whole(st):
            return st[:, :]

        fc1_staged, fc2_staged, exp_staged, l1_staged = {}, {}, {}, {}
        for j in range(HC + 2):
            if j < HC:
                fc1_staged[j] = stage_weights([(blocks((0, KC)), lambda e, s, j=j: fc1_w[j])],
                                              wa[:, j, 0, 0:KC, :], wa[:, j, 1, 0:KC, :], max(j - 3, -1))
            if j >= 2:
                fc2_staged[j - 2] = stage_weights(
                    [(blocks((0, SH)), lambda e, s, j=j - 2: fc2_w[j]),
                     (blocks((SH, KC)), lambda e, s, j=j - 2: exp_w[bass.ds(e[0], 1), :, j:j + 1, :]
                      .rearrange("e p a n -> p (e a) n"))],
                    wa[:, j - 2, 0, KC:NB, :], wa[:, j - 2, 1, KC:NB, :], j - 2)
        for b in range(B):
            if b:
                for q in range(0, HC, KC):
                    t = HALVES * b - 1
                    n = stage_weights([(blocks((0, KC)), lambda e, s, b=b, q=q:
                                        exp_w[bass.ds(e[b], 1), :, q:q + KC, :].rearrange("e p a n -> p (e a) n"))],
                                      wa[:, q:q + KC, 0, NB - 1, :], wa[:, q:q + KC, 1, NB - 1, :],
                                      HC * t + q + KC + 3, (s_fc2, HC * t + q + KC))
                    for j in range(q, q + KC):
                        exp_staged[b, j] = n
            for c in range(KC):
                l1_staged[b] = stage_weights(
                    [(whole, lambda e, s, b=b, c=c: l1_w[bass.ds(s[b], 1), :, c:c + 1, :]
                      .rearrange("e p c n -> p (e c n)"))],
                    l1_hl[:, c, 0, :], l1_hl[:, c, 1, :],
                    HALVES * HC * b + L1_UNIT + KC + c if b else HC + c // 2,
                    (s_pe["L1"], KC * HALVES * b) if b else (s_stlo, EARLY))
        b_staged = {}
        for name, dram, hl, kib, n_in in (("WG", wg, wg_hl, 32, 2 * KC), ("N1", wn1, wn1_hl, 64, 1),
                                          ("SO", wsoma, wsoma_hl, 96, KC), ("TE", wtemp, wtemp_hl, 184, KC),
                                          ("OU", wout, wout_hl, 112, KC)):
            for c in range(n_in):
                chunk = kib // CHUNK_KIB + c // 2
                src = lambda e, s, d=dram, c=c: d[:, c, :]
                if name == "N1":
                    hi, lo = [hl[:, a, :, :].rearrange("p c n -> p (c n)") for a in range(2)]
                    src = lambda e, s, d=dram: d.rearrange("p c n -> p (c n)")
                else:
                    hi, lo = hl[:, c, 0, :], hl[:, c, 1, :]
                unit, free = UNITS - HC + chunk + 3, (s_fc2, UNITS - HC + chunk + 1)
                if name == "SO" and c >= 2:
                    unit = UNITS + 1
                if name == "TE":
                    free = (s_pe["L1"], KC * NT)
                if name in ("TE", "OU"):
                    unit = UNITS + 2 + (c if name == "TE" else KC + c) // 2
                b_staged[name, c] = stage_weights([(whole, src)], hi, lo, unit, free, center=name == "OU")
            b_staged[name] = b_staged[name, n_in - 1]

        def stage_of(n):
            return stage_early[n] if n < EARLY else stage[n % 2]

        staged_count, loaded = [0, 0], []
        for n, entry in enumerate(STAGES):
            if n < EARLY:
                loaded.append((s_early[n], 16 * len(entry[0])))
            else:
                staged_count[n % 2] += 16 * len(entry[0])
                loaded.append((s_st[n % 2], staged_count[n % 2]))
        centered = [n for n, entry in enumerate(STAGES) if entry[5]]
        split_behind = {}
        for n, entry in enumerate(STAGES):
            split_behind.setdefault(entry[3], []).append(n)
        assert [n for u in sorted(split_behind) for n in split_behind[u]] == list(range(len(STAGES)))

        CHUNKS = dict(L1=KC, N1=1, SO=KC, MO=1, WG=KC, TE=KC, OU=KC, SS=1, RB=1, L3=KC)
        LAG = dict(N1=0, MO=0, WG=0, SO=0, TE=1, OU=1, SS=1, RB=1, L3=2)
        READ = dict(L1=s_x2, N1=s_h1, SO=s_soma, MO=s_mod, WG=s_gated, TE=s_spk, SS=s_std, RB=s_z, L3=s_y)

        def chunk_read(k, i, m):
            if k == "fc1":
                return s_hlo, i + 1
            if k == "fc2":
                return s_x1, KC * i + m + 1
            if k == "OU":
                return (s_ssq, SH * i + m) if m else (s_sq, KC * i + 1)
            return READ[k], KC * (i + 1) if k == "RB" else CHUNKS[k] * i + m + 1

        def blended(q):
            n, d = divmod(q, TAUS)
            return (s_blend, (TAUS - 1) * n + d) if d else (s_blend0, n + 1)

        LAG.update(X2H=-1, X2L=-1, CTXH=0, CTX=0, WX=0, WGa=0, WGb=0, WGc=0, BL=0, TEMPH=0, TEMPL=0, SPK=1,
                   SPKH=1, SPKL=1, SUMSQ=1, Z=2, X3=2, X3H=2, X3L=2, W3H=2, W3L=2)
        PARTS = dict(CHUNKS, CTX=2, SUMSQ=1)

        def steps(text):
            found = []
            for word in text.split():
                name, _, parts = word.partition(".")
                k, _, i = name.partition("@")
                parts = [int(m) for m in parts] or range(PARTS.get(k, KC))
                found += [(k, int(i) if i else LAG[k], m) for m in parts]
            return found

        def behind(texts):
            return {UNITS - 5 + n: steps(text) for n, text in enumerate(texts)}

        def rounds(usual, early, first, other):
            had = set(first).union(*early.values())
            order = list(first)
            for r in range(1, NT + 2):
                for k, lag, m in steps(other.get(r, usual)):
                    step = k, r - lag, m
                    if 0 <= r - lag < NT and step not in had:
                        order.append(step)
                        had.add(step)
            return order

        LAST = NT - 1
        PE_A = behind(["", "", "N1@0", "MO@0 WG@0.0", "WG@0.1", "WG@0.2", "WG@0.3"])
        PE_ORDER = rounds(
            "N1 WX.0 MO TE WG OU L3 SS SO.01 RB SO.23",
            PE_A, steps(f"""L1@{LAST} SO@0
                            N1@1 WX@1.0 MO@1 WX@1.12 TE@0 WG@1 OU@0 SO@1.01 SS@0 SO@1.23 RB@0
                            N1@2 WX@2.0 MO@2 WX@2.12"""),
            {NT: "TE L3.01 OU L3.2 SS L3.3 RB"})
        ACT_A = behind(["X2H@0.01", "X2H@0.23 CTXH@0.01", "CTXH@0.23 N1@0", "MO@0 WG@0.0 BL@0.0", "W3H@0",
                        f"WG@0.1 X1H@{LAST} ST:SO@0.23 WG@0.2 BL@0.1 WG@0.3"])
        ACT_ORDER = rounds(
            """N1 TEMPH@1.3 MO CTXH.01 TE.0 CTXH.23 TE.1 WG.0 TE.2 BL.0 TE.3 SPKH.01 W3H WG.1 SPKH.23 WG.2
               BL.1 WG.3 X3H OU BL.2 SS SO.0 BL.3 SO.1 TEMPH.01 X2H SO.23 TEMPH.2""",
            ACT_A, steps("""BL@0.2 ST:TE@0.01 SO@0.01 X2H@1 N1@1 BL@0.3 SO@0.23 MO@1 ST:TE@0.23 TEMPH@0
                            CTXH@1 ST:OU@0.01 TE@0 ST:OU@0.23 SPKH@0"""),
            {1: """WG.0 BL.0 WG.123 OU.01 BL.1 OU.23 SO.01 BL.2 SS X2H SO.23 N1@-1 TEMPH.01 BL.3 TEMPH.2""",
             NT: "TEMPH@1.3 W3H TE.0 X3H.01 TE.1 X3H.23 TE.23 SPKH OU SS"})
        V_A = behind(["X2L@0.01", "X2L@0.23 CTX@0.0", "CTX@0.1", "WGa@0.0", "WGb@0.0 WGc@0.0 W3L@0",
                      f"X1@{LAST} X1L@{LAST} ST:SO@0.23 WG@0.1"])
        V_ORDER = rounds(
            """Z X3 CTX SPK.01 WGa.0 SPK.2 WGb.0 WGc.0 SPK.3 SPKL W3L WG.1 X3L WGa.2 SUMSQ WGb.2 WGc.2 L3 SS
               WGa.3 WGb.3 X2L WGc.3 TEMPL""",
            V_A, steps(f"""WGa@0.2 L1@{LAST}.01 WGb@0.2 WGc@0.2 L1@{LAST}.23 X2L@1 ST:TE@0.01 WG@0.3
                           ST:TE@0.23 TEMPL@0 CTX@1 CEN:OU@0.01 ST:OU@0.01 SPK@0.01 CEN:OU@0.2 SPK@0.2
                           CEN:OU@0.3 SPK@0.3 ST:OU@0.23 SPKL@0"""),
            {1: "WG.01 SUMSQ WGa.2 SS WGb.2 X2L WGc.2 WG.3 TEMPL",
             NT: "Z X3 SPK.0 W3L X3L.01 SPK.1 X3L.23 SPK.23 SPKL L3.01 SUMSQ L3.2 SS L3.3",
             NT + 1: "Z.0 X3.0 Z.1 X3L.0 X3.1 Z.2 X3L.1 X3.2 Z.3 X3L.2 X3.3 X3L.3 L3"})

        bank_of, before, holder = {}, {}, [None] * 8

        def take(key, n):
            bank_of[key], before[key], holder[n] = bank[n], holder[n], key

        ring = []
        for u in range(UNITS + 2):
            t, j = divmod(u, HC)
            if u < UNITS:
                ring.append(("fc1", u, 0))
            if 0 < t < NT and L1_UNIT <= j < L1_UNIT + KC:
                ring.append(("L1", t - 1, j - L1_UNIT))
            ring += PE_A.get(u, [])
        for n, key in enumerate(ring):
            take(key, KC + n % KC)
        for n in range(KC):
            holder[n] = ("fc2", NT - 1, n)
        waiting = list(range(KC)) + [KC + (len(ring) + q) % KC for q in range(KC)]
        begun = set()
        for k, i, m in PE_ORDER:
            key = ("WG" if k == "WX" else k, i, m)
            if key in bank_of:
                begun.discard(key)
                n = holder.index(key)
            else:
                def late(n):
                    if holder[n][0] == "WG" and holder[n][2] == KC - 1:
                        return (k in ("L3", "SS", "SO", "RB") or
                                i in (1, 2) and (k == "N1" or key[0] == "WG" and m == 0))
                    return holder[n] in begun or k in ("N1", "WX", "MO", "TE") and holder[n][0] == "RB"

                n = next(n for n in waiting if not late(n))
                take(key, n)
                if k == "WX":
                    begun.add(key)
            waiting.remove(n)
            waiting.append(n)

        block = ctx.enter_context(nc.Block())

        @block.sync
        def _(eng):
            wait = Waits(eng)

            def load_part(n, part):
                columns_of, source = STAGES[n][0][part]
                eng.dma_start(columns_of(stage_of(n)), source(expert, subject)).then_inc(loaded[n][0], 16)

            def load_stage(n):
                wait(s_stlo, n - 1)
                for part in range(len(STAGES[n][0])):
                    load_part(n, part)

            expert = subject = None
            eng.dma_start(idx[0:1, 0:B], tok16).then_inc(s_idx, 16)
            eng.dma_start(idx[0:1, B:2 * B], tok8).then_inc(s_idx, 16)
            load_part(0, 0)
            for c in range(KC):
                eng.dma_start(x_raw[0][:, c, :], x[0, :, c, :]).then_inc(s_x0[c], 16)
            load_part(1, 0)
            load_part(2, 0)
            wait(s_idx, 32)
            expert = [nc.sync.value_load(idx[0:1, b:b + 1], min_val=0, max_val=EXPERTS - 1) for b in range(B)]
            subject = [nc.sync.value_load(idx[0:1, B + b:B + b + 1], min_val=0, max_val=SUBJECTS - 1)
                       for b in range(B)]
            for n in range(3, EARLY + 2):
                for part in range(len(STAGES[n][0])):
                    load_part(n, part)

            def load_x(t):
                if t >= 2:
                    wait(s_x2st, 16 * (t - 1))
                eng.dma_start(x_raw[t % 2][:, :, :], x[t]).then_inc(s_xld[t % 2], 16)

            def store_x2(t):
                wait(s_x2, KC * (t + 1))
                eng.dma_start(x2_dram[t], x_raw[t % 2][:, :, :]).then_inc(s_x2st, 16)

            def load_xt_part(i, c):
                eng.dma_start(xt[i % 3][:, c, :], x2_dram[i, :, c, :]).then_inc(s_xt[i % 3][c], 16)

            def load_xt(i):
                if i == 0:
                    wait(s_x2st, 16 * (NT - 1))
                elif i == 1:
                    wait(s_pe["L1"], KC * NT)
                else:
                    wait(s_x2st, 16 * NT)
                for c in range(KC):
                    load_xt_part(i, c)

            def load_l3w(b):
                if b:
                    wait(s_pe["L3"], KC * HALVES * b)
                else:
                    wait(s_fc2, UNITS - HC + 2)
                eng.dma_start(l3w_raw[:, :, 1, :], l3_w[bass.ds(expert[b], 1), :, :, :]
                              .rearrange("e p c n -> p (e c) n")).then_inc(s_l3w, 16)

            transfers = [(STAGES[n - 2][3], lambda n=n: load_stage(n)) for n in range(EARLY + 2, len(STAGES))]
            transfers.append((3, lambda: load_x(1)))
            for t in range(NT - 1):
                done = HC * (t + 1) + L1_UNIT + KC
                transfers.append((done, lambda t=t: store_x2(t)))
                if t + 2 < NT:
                    transfers.append((done + 0.5, lambda t=t: load_x(t + 2)))

            transfers.append((UNITS - HC + L1_UNIT + KC + 0.5, lambda: load_xt(0)))
            transfers.append((UNITS - HC + L1_UNIT + KC + 0.6, lambda: load_l3w(0)))
            transfers.append((UNITS + 1, lambda: load_xt(1)))
            transfers.append((UNITS + 1.5, lambda: store_x2(NT - 1)))
            transfers.append((UNITS + 2.5, lambda: load_xt(2)))
            for _, transfer in sorted(transfers, key=lambda v: v[0]):
                transfer()
            for r in range(NT + 2):
                i = r - LAG["L3"]
                if i < 0:
                    continue
                if i % HALVES == HALVES - 1 and i + 1 < NT:
                    load_l3w((i + 1) // HALVES)
                for c in range(KC):
                    wait(s_y, KC * i + c + 1)
                    eng.dma_start(out[i, :, c, :], xt[i % 3][:, c, :]).then_inc(s_out[c], 16)
                    if c and i + 3 < NT:
                        wait(s_out[c - 1], 16 * (i + 1))
                        load_xt_part(i + 3, c - 1)
                if i + 3 < NT:
                    wait(s_out[KC - 1], 16 * (i + 1))
                    load_xt_part(i + 3, KC - 1)
            for c in range(KC):
                wait(s_out[c], 16 * NT)
            wait(s_x2st, 16 * NT)

        @block.gpsimd
        def _(eng):
            wait = Waits(eng)
            eng.dma_start(small_sb[:, :], small).then_inc(s_small, 16)
            eng.memset(ident[:, :], 0.0).then_inc(s_id, 1)
            wait(s_id, 1)
            eng.affine_select(out=ident[:, :], in_=ident[:, :], compare_op=ALU.not_equal, fill=1.0, base=0,
                              pattern=[[-1, P]], channel_multiplier=1).then_inc(s_id, 1)
            wait(s_idx, 32)
            expert = [nc.gpsimd.value_load(idx[0:1, b:b + 1], min_val=0, max_val=EXPERTS - 1) for b in range(B)]
            subject = [nc.gpsimd.value_load(idx[0:1, B + b:B + b + 1], min_val=0, max_val=SUBJECTS - 1)
                       for b in range(B)]
            for b in range(B):
                eng.dma_start(exp_b_sb[:, b:b + 1], exp_b[bass.ds(expert[b], 1), :].rearrange("e p -> p e")
                              ).then_inc(s_pick, 16)
                eng.dma_start(l1_b_sb[:, b * KC:(b + 1) * KC],
                              l1_b[bass.ds(subject[b], 1), :, :].rearrange("e p c -> p (e c)")
                              ).then_inc(s_pick, 16)
                eng.dma_start(l3_b_sb[:, b * KC:(b + 1) * KC],
                              l3_b[bass.ds(expert[b], 1), :, :].rearrange("e p c -> p (e c)")
                              ).then_inc(s_pick, 16)
            for i in range(NT):
                wait(s_mod, i + 1)
                eng.dma_start(mod_dram[i], mod_row[0:TAUS, :]).then_inc(s_mst, 16)
                wait(s_mst, 16 * (i + 1))
                if i:
                    wait(s_drive, KC * TAUS * i)
                else:
                    wait(s_fc2, UNITS - HC + 10)
                eng.dma_start(mod_t[:, :, :], mod_dram[i:i + 1, :, :].to_broadcast([P, TAUS, TOK])
                              ).then_inc(s_mld, 16)

        @block.scalar
        def _(eng):
            wait = Waits(eng)

            def stage_hi(n):
                parts, hi, _, _, free, center = STAGES[n]
                wait(*loaded[n])
                if center:
                    wait(s_cen, 3 * (centered.index(n) + 1))
                if free:
                    wait(*free)
                src = stage_of(n)[:, :]
                if len(hi.shape) == 3:
                    src = src.rearrange("p (c n) -> p c n", n=P)
                eng.activation(hi, src, ACT.Copy).then_inc(s_sthi, 1)

            def x_hi(t, c):
                if t:
                    wait(s_xld[t % 2], 16 * ((t + 1) // 2))
                else:
                    wait(s_x0[c], 16)
                if t >= 2:
                    wait(s_pe["L1"], KC * (t - 1))
                eng.activation(x_hl[t % 2][:, 0, c, :], x_raw[t % 2][:, c, :], ACT.Copy).then_inc(s_xhi, 1)

            def x1_hi(t, c):
                wait(s_x1, KC * t + c + 1)
                wait(s_fc1, HC * (t + 1))
                eng.activation(x_hl[t % 2][:, 0, c, :], x_raw[t % 2][:, c, :], ACT.Copy).then_inc(s_x1hi, 1)

            def x2_hi(i, c):
                wait(s_xt[i % 3][c], 16 * (i // 3 + 1))
                if i and c < SH:
                    wait(s_x2free, SH * (i - 1) + c + 1)
                elif i:
                    wait(s_pe["SO"], KC * i)
                else:
                    wait(s_fc2, UNITS - HC + 4)
                eng.activation(x2_hl[:, 0, c, :], xt[i % 3][:, c, :], ACT.Copy).then_inc(s_x2hi, 1)

            def step(k, i, m):
                if k == "X2H":
                    return x2_hi(i, m)
                if k == "X1H":
                    return x1_hi(i, m)
                if k.startswith("ST:"):
                    return stage_hi(b_staged[k[3:], m] - 1)
                n = CHUNKS.get(k, KC) * i + m
                if k in CHUNKS:
                    ps = bank_of[k, i, m]
                    wait(s_pe[k], n + 1)
                if k == "SS":
                    if i:
                        wait(s_rstd, i)
                    eng.activation(std[:, :], ps[:, 0:TOK // P], ACT.Sqrt, bias=eps_sb[:, 0:1],
                                   scale=1.0 / DIM).then_inc(s_std, 1)
                elif k == "CTXH":
                    wait(s_ctx, n + 1)
                    if i:
                        wait(s_pe["WG"], KC * i)
                    else:
                        wait(s_pe["L1"], KC * (NT - 1))
                    if i >= 2:
                        wait(s_x3, KC * (i - 1))
                    eng.activation(ctx_hi[:, m, :], ctx_raw[:, m, :], ACT.Copy).then_inc(s_ctxhi, 1)
                elif k == "N1":
                    if i:
                        wait(s_mst, 16 * i)
                    else:
                        wait(s_fc2, UNITS - HC + 9)
                    if i > 2:
                        wait(s_pe["L3"], KC * (i - 2))
                    eng.activation(h1[:, :], ps[:, :], ACT.Gelu, bias=bn1_sb[:, 0:1]).then_inc(s_h1, 1)
                elif k == "MO":
                    eng.activation(mod_row[0:TAUS, :], ps[0:TAUS, :], ACT.Tanh, bias=bn2_sb[0:TAUS, 0:1],
                                   scale=0.5).then_inc(s_mod, 1)
                elif k == "WG":
                    eng.activation(ps[:, :], ps[:, :], ACT.Tanh, bias=bg_sb[:, m:m + 1],
                                   scale=0.5).then_inc(s_wgt, 1)
                elif k == "TEMPH":
                    wait(s_x2st, 16 * NT)
                    wait(*blended(TAUS * n + TAUS - 1))
                    if i:
                        wait(s_pe["OU"], KC * i)
                    eng.activation(ts_hi[:, m, :], temporal[:, m, :], ACT.Copy).then_inc(s_temphi, 1)
                elif k == "TE":
                    eng.activation(ps[:, :], ps[:, :], ACT.Tanh, bias=btemp_sb[:, m:m + 1],
                                   scale=0.5).then_inc(s_gate, 1)
                elif k == "SPKH":
                    wait(s_spk, n + 1)
                    wait(s_pe["TE"], KC * (i + 1))
                    eng.activation(ts_hi[:, m, :], soma[:, m, :], ACT.Copy).then_inc(s_spkhi, 1)
                elif k == "SO":
                    if i:
                        wait(s_pe["OU"], KC * i)
                    eng.activation(soma[:, m, :], ps[:, :], ACT.Gelu,
                                   bias=bsoma_sb[:, m:m + 1]).then_inc(s_soma, 1)
                elif k == "OU":
                    wait(s_pe["WG"], KC * min(i + 2, NT))
                    eng.activation(o_sb[:, m, :], ps[:, :], ACT.Copy).then_inc(s_o, 1)
                    wait(s_o, n + 1)
                    if m == 0 and i:
                        wait(s_pe["SS"], i)
                    eng.activation(sumsq[:, :] if m == 0 else ps[:, :], ps[:, :], ACT.Square).then_inc(s_sq, 1)
                elif k == "BL":
                    wait(s_trace, TAUS * n + 1)
                    if i:
                        wait(s_pe["TE"], KC * i)
                    eng.activation(temporal[:, m, :], drive[TAUS * n % 2][:, :], ACT.Identity,
                                   scale=blend_sb[:, TAUS * m:TAUS * m + 1]).then_inc(s_blend0, 1)
                elif k == "W3H":
                    if i % HALVES == 0:
                        wait(s_l3w, 16 * (i // HALVES + 1))
                        eng.activation(l3w_hl[:, m, 0, :], l3w_raw[:, m, 1, :], ACT.Copy).then_inc(s_w3hi, 1)
                elif k == "X3H":
                    wait(s_x3, n + 1)
                    wait(s_pe["WG"], KC * min(i + 3, NT))
                    if i:
                        wait(s_pe["L3"], KC * i)
                    eng.activation(x3_hi[m][:, :], xt[i % 3][:, m, :], ACT.Copy).then_inc(s_x3hi, 1)

            stage_hi(0)
            for c in range(KC):
                x_hi(0, c)
            for n in split_behind[-1][1:]:
                stage_hi(n)
            wait(s_small, 16)
            for u in range(UNITS + 1):
                t, j = divmod(u, HC)
                if u < UNITS:
                    ps = bank_of["fc1", u, 0]
                    wait(s_fc1, u + 1)
                    eng.activation(ps[:, :], ps[:, :], ACT.Gelu, bias=fc1_b_sb[:, j:j + 1]).then_inc(s_gelu, 1)
                    wait(s_gelu, u + 1)
                    if u >= 2:
                        wait(s_fc2, u - 1)
                    eng.activation(h_hl[u % 2][:, 0, :], ps[:, :], ACT.Copy).then_inc(s_hhi, 1)
                if t and t < NT and j in (2, 3):
                    x1_hi(t - 1, 2 * (j - 2))
                    x1_hi(t - 1, 2 * (j - 2) + 1)
                for n in split_behind.get(u, []):
                    stage_hi(n)
                for now in ACT_A.get(u, []):
                    step(*now)
                if u == CONST_UNIT:
                    eng.activation(alpha[:, :], tau_sb, ACT.Exp).then_inc(s_exp, 1)
                    wait(s_cst, 2)
                    eng.activation(blend_sb, blend_sb, ACT.Exp).then_inc(s_exp, 1)
                if SPLIT_UNIT <= j < SPLIT_UNIT + KC and t + 1 < NT:
                    x_hi(t + 1, j - SPLIT_UNIT)

            for now in ACT_ORDER:
                step(*now)

        @block.tensor
        def _(eng):
            wait = Waits(eng)

            def split_product(ps, w_hi, w_lo, x_hi, x_lo, first, last):
                eng.matmul(ps, w_hi, x_hi, start=first, stop=False)
                eng.matmul(ps, w_hi, x_lo, start=False, stop=False)
                return eng.matmul(ps, w_lo, x_hi, start=False, stop=last)

            def bank_free(key):
                if before[key]:
                    wait(*chunk_read(*before[key]))

            def fc1(u):
                t, j = divmod(u, HC)
                wait(s_stlo, fc1_staged[j])
                bank_free(("fc1", u, 0))
                for c in range(KC):
                    wait(s_xlo, KC * t + c + 1)
                    mm = split_product(bank_of["fc1", u, 0][:, :], wa[:, j, 0, c, :], wa[:, j, 1, c, :],
                                       x_hl[t % 2][:, 0, c, :], x_hl[t % 2][:, 1, c, :], c == 0, c == KC - 1)
                mm.then_inc(s_fc1, 1)

            def fc2(u):
                t, j = divmod(u, HC)
                wait(s_hlo, u + 1)
                b = t // HALVES
                wait(s_stlo, exp_staged[b, j] if b else fc2_staged[j])
                for m in range(KC):
                    if j == 0 and t:
                        wait(s_x1, KC * (t - 1) + m + 1)
                    mm = split_product(acc[m][:, :], wa[:, j, 0, KC + m, :], wa[:, j, 1, KC + m, :],
                                       h_hl[u % 2][:, 0, :], h_hl[u % 2][:, 1, :], j == 0, j == HC - 1)
                mm.then_inc(s_fc2, 1)

            def l1(t, m):
                bank_free(("L1", t, m))
                ps = bank_of["L1", t, m]
                wait(s_stlo, l1_staged[t // HALVES])
                wait(s_x1lo, KC * (t + 1))
                for c in range(KC):
                    mm = split_product(ps[:, :], l1_hl[:, c, 0, m * P:(m + 1) * P],
                                       l1_hl[:, c, 1, m * P:(m + 1) * P], x_hl[t % 2][:, 0, c, :],
                                       x_hl[t % 2][:, 1, c, :], c == 0, c == KC - 1)
                mm.then_inc(s_pe["L1"], 1)

            def split_terms(k, i, m, cs):
                n_in = 2 * KC if k == "WG" else KC
                for c in cs:
                    if k == "N1":
                        w_hi, w_lo = wn1_hl[:, 0, c, :], wn1_hl[:, 1, c, :]
                    else:
                        w_hl = dict(WG=wg_hl, SO=wsoma_hl, TE=wtemp_hl, OU=wout_hl, L3=l3w_hl)[k]
                        w_hi, w_lo = w_hl[:, c, 0, m * P:(m + 1) * P], w_hl[:, c, 1, m * P:(m + 1) * P]
                    if k == "TE":
                        wait(s_templo, KC * i + c + 1)
                        v_hi, v_lo = ts_hi[:, c, :], temporal_lo[:, c, :]
                    elif k == "OU":
                        wait(s_spklo, KC * i + c + 1)
                        v_hi, v_lo = ts_hi[:, c, :], spikes_lo[:, c, :]
                    elif k == "L3":
                        wait(s_x3lo, KC * i + c + 1)
                        v_hi, v_lo = x3_hi[c][:, :], x3_lo[c][:, :]
                    elif c >= KC:
                        wait(s_ctxlo, KC * i + c - KC + 1)
                        v_hi, v_lo = ctx_hi[:, c - KC, :], ctx_lo[:, c - KC, :]
                    else:
                        wait(s_x2lo, KC * i + c + 1)
                        v_hi, v_lo = x2_hl[:, 0, c, :], x2_hl[:, 1, c, :]
                    mm = split_product(bank_of[k, i, m][:, :], w_hi, w_lo, v_hi, v_lo,
                                       c == 0, c == n_in - 1)
                return mm

            def step(k, i, m):
                b = i // HALVES
                if k == "WX":
                    wait(s_stlo, b_staged["WG"])
                    bank_free(("WG", i, m))
                    split_terms("WG", i, m, range(KC))
                    return
                ps = bank_of[k, i, m]
                if k == "WG" and ("WX", i, m) in PE_ORDER:
                    split_terms(k, i, m, range(KC, 2 * KC)).then_inc(s_pe[k], 1)
                    return
                if k == "L3":
                    wait(s_w3lo, KC * (b + 1))
                if k == "L3" and i == NT - 1:
                    if m == 0:
                        for a in range(KC):
                            bank_free((k, i, a))
                        for c in range(KC):
                            for a in range(KC):
                                mm = split_terms(k, i, a, [c])
                                if c == KC - 1:
                                    mm.then_inc(s_pe[k], 1)
                    return
                if k == "SO" and m >= 2:
                    if m == 2:
                        wait(s_stlo, b_staged[k])
                        bank_free((k, i, 2))
                        bank_free((k, i, 3))
                        for c in range(KC):
                            for a in (2, 3):
                                mm = split_terms(k, i, a, [c])
                                if c == KC - 1:
                                    mm.then_inc(s_pe[k], 1)
                            if c < KC - 1:
                                mm.then_inc(s_x2free, 1)
                    return
                if k == "L1":
                    l1(i, m)
                    return
                bank_free((k, i, m))
                if k in b_staged:
                    wait(s_stlo, b_staged[k])
                    split_terms(k, i, m, range(2 * KC if k == "WG" else KC)).then_inc(s_pe[k], 1)
                elif k == "MO":
                    wait(s_h1, i + 1)
                    eng.matmul(ps[0:TAUS, :], wn2_sb, h1[:, :], start=True, stop=True).then_inc(s_pe[k], 1)
                elif k == "SS":
                    wait(s_cst, 1)
                    wait(s_ssq, SH * (i + 1))
                    for q in range(TOK // P):
                        mm = eng.matmul(ps[:, q:q + 1], sumsq[:, q * P:(q + 1) * P], ones[:, 0:1],
                                        start=True, stop=True)
                    mm.then_inc(s_pe[k], 1)
                elif k == "RB":
                    for q in range(TOK // P):
                        wait(s_diag, (TOK // P) * i + q + 1)
                        mm = eng.matmul(ps[:, q * P:(q + 1) * P], ones[:, :], diag[:, q, :],
                                        start=True, stop=True)
                    mm.then_inc(s_pe[k], 1)
                elif k == "L3":
                    split_terms(k, i, m, range(KC)).then_inc(s_pe[k], 1)

            for u in range(UNITS + 2):
                t, j = divmod(u, HC)
                if u < UNITS:
                    fc1(u)
                if u >= 2:
                    fc2(u - 2)
                if 0 < t < NT and L1_UNIT <= j < L1_UNIT + KC:
                    l1(t - 1, j - L1_UNIT)
                for now in PE_A.get(u, []):
                    step(*now)
            for now in PE_ORDER:
                step(*now)

        @block.vector
        def _(eng):
            wait = Waits(eng)

            def low_part(lo, raw, hi):
                return eng.tensor_tensor(lo, raw, hi.bitcast(F32), ALU.subtract)

            def stage_lo(n):
                _, hi, lo, _, _, _ = STAGES[n]
                st = stage_of(n)
                src = st[:, :]
                if len(lo.shape) == 3:
                    src = src.rearrange("p (c n) -> p c n", n=P)
                wait(s_sthi, n + 1)
                low_part(lo, src, hi).then_inc(s_stlo, 1)

            def center_stage(n):
                st, q = stage_of(n), 3 * centered.index(n)
                wait(*loaded[n])
                eng.tensor_reduce(wout_mean[:, :], st[:, :], AX.X, ALU.add).then_inc(s_cen, 1)
                wait(s_cen, q + 1)
                eng.tensor_scalar(wout_mean[:, :], wout_mean[:, :], 1.0 / DIM, None, ALU.mult).then_inc(s_cen, 1)
                wait(s_cen, q + 2)
                eng.tensor_scalar(st[:, :], st[:, :], wout_mean[:, 0:1], 0.5, ALU.subtract, ALU.mult
                                  ).then_inc(s_cen, 1)
                wait(s_cen, q + 3)

            def x_lo(t, c):
                wait(s_xhi, KC * t + c + 1)
                low_part(x_hl[t % 2][:, 1, c, :], x_raw[t % 2][:, c, :], x_hl[t % 2][:, 0, c, :]
                         ).then_inc(s_xlo, 1)

            def x1_lo(t, c):
                wait(s_x1hi, KC * t + c + 1)
                low_part(x_hl[t % 2][:, 1, c, :], x_raw[t % 2][:, c, :], x_hl[t % 2][:, 0, c, :]
                         ).then_inc(s_x1lo, 1)

            def x1_of(t, m):
                wait(s_fc2, HC * (t + 1))
                bias = fc2_b_sb[:, m:m + 1] if m < SH else exp_b_sb[:, t // HALVES:t // HALVES + 1]
                xr = x_raw[t % 2][:, m, :]
                eng.scalar_tensor_tensor(xr, acc[m][:, :], bias, xr, ALU.add, ALU.add).then_inc(s_x1, 1)

            def x2_of(t, m):
                ps = bank_of["L1", t, m]
                wait(s_pe["L1"], KC * t + m + 1)
                b = t // HALVES
                xr = x_raw[t % 2][:, m, :]
                eng.scalar_tensor_tensor(xr, ps[:, :], l1_b_sb[:, b * KC + m:b * KC + m + 1], xr, ALU.add, ALU.add
                                         ).then_inc(s_x2, 1)

            def x2_lo(i, c):
                wait(s_x2hi, KC * i + c + 1)
                low_part(x2_hl[:, 1, c, :], xt[i % 3][:, c, :], x2_hl[:, 0, c, :]).then_inc(s_x2lo, 1)

            def constants():
                wait(s_small, 16)
                eng.tensor_scalar(bg_sb, bg_sb, 0.5, None, ALU.mult)
                eng.tensor_scalar(bn2_sb[0:TAUS, :], bn2_sb[0:TAUS, :], 0.5, None, ALU.mult)
                eng.tensor_scalar(btemp_sb, btemp_sb, 0.5, None, ALU.mult)
                blend_v = blend_sb.rearrange("p (c d) -> p c d", d=TAUS)
                links = [0]

                def link(ins):
                    links[0] += 1
                    ins.then_inc(s_chain, 1)
                    wait(s_chain, links[0])

                link(eng.tensor_reduce(blend_max[:, :], blend_v, AX.X, ALU.max))
                for c in range(KC):
                    ins = eng.tensor_scalar(blend_v[:, c, :], blend_v[:, c, :], blend_max[:, c:c + 1], None,
                                            ALU.subtract)
                ins.then_inc(s_cst, 1)
                wait(s_exp, 2)
                link(eng.tensor_reduce(blend_max[:, :], blend_v, AX.X, ALU.add))
                link(eng.reciprocal(blend_max[:, :], blend_max[:, :]))
                for c in range(KC):
                    eng.tensor_scalar(blend_v[:, c, :], blend_v[:, c, :], blend_max[:, c:c + 1], 0.25,
                                      ALU.mult, ALU.mult)
                link(eng.tensor_scalar(alpha[:, :], alpha[:, :], 1.0, None, ALU.add))
                link(eng.reciprocal(alpha[:, :], alpha[:, :]))

            def step(k, i, m):
                b = i // HALVES
                xi = xt[i % 3]
                first_half = i % HALVES == 0
                n = KC * i + m
                if k == "L1":
                    x2_of(i, m)
                elif k == "X1":
                    x1_of(i, m)
                elif k == "X1L":
                    x1_lo(i, m)
                elif k.startswith("CEN:"):
                    center_stage(b_staged[k[4:], m] - 1)
                elif k.startswith("ST:"):
                    stage_lo(b_staged[k[3:], m] - 1)
                elif k == "X2L":
                    x2_lo(i, m)
                elif k == "SS":
                    wait(s_std, i + 1)
                    eng.reciprocal(rstd[:, :], std[:, :]).then_inc(s_rstd, 1)
                    wait(s_rstd, i + 1)
                    wait(s_id, 2)
                    if i:
                        wait(s_pe["L3"], KC * i)
                    for q in range(TOK // P):
                        eng.tensor_scalar(diag[:, q, :], ident[:, :], rstd[:, q:q + 1], None, ALU.mult
                                          ).then_inc(s_diag, 1)
                elif k == "Z":
                    wait(s_pe["RB"], i + 1)
                    wait(s_o, n + 1)
                    eng.scalar_tensor_tensor(o_sb[:, m, :], o_sb[:, m, :], gamma_sb[:, m:m + 1],
                                             bank_of["RB", i, 0][:, :], ALU.mult, ALU.mult).then_inc(s_z, 1)
                elif k == "X3":
                    wait(s_z, n + 1)
                    eng.scalar_tensor_tensor(xi[:, m, :], o_sb[:, m, :], beta_sb[:, m:m + 1], xi[:, m, :],
                                             ALU.add, ALU.add).then_inc(s_x3, 1)
                elif k == "X3L":
                    wait(s_x3hi, n + 1)
                    if m == KC - 1:
                        wait(s_mst, 16 * min(i + 3, NT))
                    low_part(x3_lo[m][:, :], xi[:, m, :], x3_hi[m][:, :]).then_inc(s_x3lo, 1)
                elif k == "W3L":
                    if i % HALVES == 0:
                        wait(s_w3hi, KC * b + m + 1)
                        low_part(l3w_hl[:, m, 1, :], l3w_raw[:, m, 1, :], l3w_hl[:, m, 0, :]).then_inc(s_w3lo, 1)
                elif k == "CTX":
                    def context_of(c):
                        start = 0.0
                        if not first_half:
                            wait(s_ctxl, KC * (i // HALVES) + c + 1)
                            start = ctx_last[:, c:c + 1]
                        wait(s_xt[i % 3][c], 16 * (i // 3 + 1))
                        eng.tensor_tensor_scan(ctx_raw[:, c, :], alpha[:, 0:1].to_broadcast([P, TOK]),
                                               xi[:, c, :], start, ALU.mult, ALU.add).then_inc(s_ctx, 1)

                    def keep_last(c):
                        if first_half:
                            wait(s_ctx, KC * i + c + 1)
                            eng.tensor_copy(ctx_last[:, c:c + 1], ctx_raw[:, c, TOK - 1:TOK]).then_inc(s_ctxl, 1)

                    def context_lo(c):
                        wait(s_ctxl, KC * (i // HALVES) + c + 1)
                        wait(s_ctxhi, KC * i + c + 1)
                        low_part(ctx_lo[:, c, :], ctx_raw[:, c, :], ctx_hi[:, c, :]).then_inc(s_ctxlo, 1)

                    if i:
                        wait(s_pe["WG"], KC * i)
                    else:
                        wait(s_pe["L1"], KC * (NT - 1))
                    if i > 2:
                        wait(s_pe["L3"], KC * (i - 2))
                    for half in (context_of, keep_last, context_lo):
                        half(2 * m)
                        half(2 * m + 1)
                elif k == "SPK":
                    wait(s_gate, n + 1)
                    wait(s_soma, n + 1)
                    eng.scalar_tensor_tensor(soma[:, m, :], bank_of["TE", i, m][:, :], 1.0, soma[:, m, :],
                                             ALU.add, ALU.mult).then_inc(s_spk, 1)
                elif k == "SPKL":
                    wait(s_spkhi, n + 1)
                    low_part(spikes_lo[:, m, :], soma[:, m, :], ts_hi[:, m, :]).then_inc(s_spklo, 1)
                elif k[:2] == "WG":
                    c = m

                    def gated_of():
                        wait(s_wgt, n + 1)
                        if n:
                            wait(s_drive, TAUS * n)
                        else:
                            wait(s_fc2, UNITS - HC + 12)
                        eng.scalar_tensor_tensor(gated[:, :], bank_of["WG", i, c][:, :], 1.0, xi[:, c, :],
                                                 ALU.add, ALU.mult).then_inc(s_gated, 1)
                        wait(s_gated, n + 1)
                        wait(s_mld, 16 * (i + 1))

                    def drive_of(d):
                        q = TAUS * n + d
                        if q >= 2:
                            wait(*blended(q - 2))
                        if d == 2 and first_half:
                            wait(s_tracel, TAUS * KC * (i // HALVES) + TAUS * c + 1)
                        eng.scalar_tensor_tensor(drive[q % 2][:, :], mod_t[:, d, :], 2.0, gated[:, :],
                                                 ALU.add, ALU.mult).then_inc(s_drive, 1)

                    def trace_of(d):
                        q = TAUS * n + d
                        wait(s_drive, q + 1)
                        start = 0.0
                        if not first_half:
                            wait(s_tracel, TAUS * KC * (i // HALVES) + TAUS * c + d + 1)
                            start = trace_last[:, TAUS * c + d:TAUS * c + d + 1]
                        eng.tensor_tensor_scan(drive[q % 2][:, :], alpha[:, 1 + d:2 + d].to_broadcast([P, TOK]),
                                               drive[q % 2][:, :], start, ALU.mult, ALU.add
                                               ).then_inc(s_trace, 1)

                    def blend_of(d):
                        q = TAUS * n + d
                        wait(s_trace, q + 1)
                        tr, te = drive[q % 2], temporal[:, c, :]
                        if first_half:
                            eng.tensor_copy(trace_last[:, TAUS * c + d:TAUS * c + d + 1],
                                            tr[:, TOK - 1:TOK]).then_inc(s_tracel, 1)
                        if d:
                            wait(*blended(q - 1))
                            eng.scalar_tensor_tensor(te, tr[:, :], blend_sb[:, TAUS * c + d:TAUS * c + d + 1],
                                                     te, ALU.mult, ALU.add).then_inc(s_blend, 1)

                    if k in ("WG", "WGa"):
                        gated_of()
                        drive_of(0)
                        drive_of(1)
                        trace_of(0)
                        trace_of(1)
                        blend_of(0)
                    if k in ("WG", "WGb"):
                        drive_of(2)
                        trace_of(2)
                        blend_of(1)
                        drive_of(3)
                    if k in ("WG", "WGc"):
                        trace_of(3)
                        blend_of(2)
                        blend_of(3)
                elif k == "SUMSQ":
                    for m in range(KC):
                        n = KC * i + m
                        wait(s_sq, n + 1)
                        if m > 1:
                            wait(s_ssq, SH * i + m - 1)
                        if m:
                            eng.tensor_tensor(sumsq[:, :], bank_of["OU", i, m][:, :], sumsq[:, :], ALU.add
                                              ).then_inc(s_ssq, 1)
                elif k == "TEMPL":
                    wait(s_temphi, n + 1)
                    low_part(temporal_lo[:, m, :], temporal[:, m, :], ts_hi[:, m, :]).then_inc(s_templo, 1)
                elif k == "L3":
                    wait(s_pe["L3"], n + 1)
                    eng.scalar_tensor_tensor(xi[:, m, :], bank_of[k, i, m][:, :],
                                             l3_b_sb[:, b * KC + m:b * KC + m + 1], xi[:, m, :],
                                             ALU.add, ALU.add).then_inc(s_y, 1)

            eng.memset(ones[:, :], 1.0)
            eng.memset(eps_sb[:, :], 1e-5).then_inc(s_cst, 1)
            stage_lo(0)
            for c in range(KC):
                x_lo(0, c)
            for n in split_behind[-1][1:]:
                stage_lo(n)

            for u in range(UNITS + 1):
                t, j = divmod(u, HC)
                if u < UNITS:
                    wait(s_hhi, u + 1)
                    if u >= 2:
                        wait(s_fc2, u - 1)
                    low_part(h_hl[u % 2][:, 1, :], bank_of["fc1", u, 0][:, :], h_hl[u % 2][:, 0, :]
                             ).then_inc(s_hlo, 1)
                if u == HC + 1:
                    wait(s_pick, 16 * 3 * B)
                if t and t < NT and j == 1:
                    for m in range(KC):
                        x1_of(t - 1, m)
                if t and t < NT and j in (2, 3):
                    x1_lo(t - 1, 2 * (j - 2))
                    x1_lo(t - 1, 2 * (j - 2) + 1)
                if t and L1_UNIT < j <= L1_UNIT + KC and t < NT:
                    m = j - 1 - L1_UNIT
                    x2_of(t - 1, m)
                for n in split_behind.get(u, []):
                    stage_lo(n)
                for now in V_A.get(u, []):
                    step(*now)
                if u == CONST_UNIT:
                    constants()
                if SPLIT_UNIT <= j < SPLIT_UNIT + KC and t + 1 < NT:
                    x_lo(t + 1, j - SPLIT_UNIT)

            for now in V_ORDER:
                step(*now)


def kernel(x, itok_B_0_15, itok_B_0_7, condB_tauraws, cond_256, condB_bn2, cond_1024, L0_cond_fc1_w,
           L0_cond_fc1_b, L0_cond_fc2_w, L0_cond_fc2_b, L0_cond_experts_w, L0_cond_experts_b,
           L1_cond_weight, L1_cond_bias, L2_cond_tau_ctx, L2_cond_Wg, L2_cond_bg, L2_cond_Wn1,
           L2_cond_bn1, L2_cond_Wsoma, L2_cond_bsoma, L2_cond_Wtemp, L2_cond_btemp, L2_cond_Wout,
           L2_cond_gamma, L2_cond_beta, L3_cond_weight, L3_cond_bias):
    import concourse.bacc as bacc
    from concourse.bass_utils import run_bass_kernel_spmd

    def a(v):
        return np.asarray(v)

    def stationary(w):
        o, i = w.shape
        return w.T.reshape(i // P, P, o).transpose(1, 0, 2)

    def columns(v):
        return v.reshape(-1, P).T

    packed = dict(
        fc1_b=columns(a(L0_cond_fc1_b)),
        fc2_b=columns(a(L0_cond_fc2_b)),
        taus=np.broadcast_to(np.concatenate([a(L2_cond_tau_ctx).reshape(1), a(condB_tauraws)]), (P, 1 + TAUS)),
        blend=a(cond_1024).reshape(TAUS, KC, P).transpose(2, 1, 0).reshape(P, KC * TAUS),
        wn2=a(cond_256).T,
        bn1=columns(a(L2_cond_bn1)),
        bn2=np.pad(a(condB_bn2).reshape(TAUS, 1), ((0, P - TAUS), (0, 0))),
        bg=columns(a(L2_cond_bg)),
        bsoma=columns(a(L2_cond_bsoma)),
        btemp=columns(a(L2_cond_btemp)),
        gamma=columns(a(L2_cond_gamma)),
        beta=columns(a(L2_cond_beta)),
    )
    data = {
        "x": a(x).reshape(B, HALVES, TOK, KC, P).transpose(0, 1, 4, 3, 2).reshape(NT, P, KC, TOK),
        "tok16": a(itok_B_0_15).reshape(1, B),
        "tok8": a(itok_B_0_7).reshape(1, B),
        "small": np.concatenate([packed[k] for k in SMALL], axis=1),
        "fc1_w": a(L0_cond_fc1_w).reshape(HC, P, KC, P).transpose(0, 3, 2, 1),
        "fc2_w": a(L0_cond_fc2_w).T.reshape(HC, P, SH, P),
        "exp_w": a(L0_cond_experts_w).reshape(EXPERTS, P, HC, P).transpose(0, 3, 2, 1),
        "exp_b": a(L0_cond_experts_b),
        "l1_w": a(L1_cond_weight).transpose(0, 2, 1).reshape(SUBJECTS, KC, P, DIM).transpose(0, 2, 1, 3),
        "l1_b": a(L1_cond_bias).reshape(SUBJECTS, KC, P).transpose(0, 2, 1),
        "wg": stationary(a(L2_cond_Wg)),
        "wn1": stationary(a(L2_cond_Wn1)),
        "wsoma": stationary(a(L2_cond_Wsoma)),
        "wtemp": stationary(a(L2_cond_Wtemp)),
        "wout": stationary(a(L2_cond_Wout)),
        "l3_w": a(L3_cond_weight).reshape(EXPERTS, KC, P, DIM).transpose(0, 2, 1, 3),
        "l3_b": a(L3_cond_bias).reshape(EXPERTS, KC, P).transpose(0, 2, 1),
    }
    nc = bacc.Bacc("TRN2", target_bir_lowering=False, num_devices=1)
    arrays, args = {}, []
    for name, v in data.items():
        arrays["in_" + name] = np.ascontiguousarray(v)
        args.append(nc.dram_tensor("in_" + name, v.shape, mybir.dt.from_np(v.dtype), kind="ExternalInput").ap())
    args.append(nc.dram_tensor("out", [NT, P, KC, TOK], F32, kind="ExternalOutput").ap())
    build(nc, *args)
    r = run_bass_kernel_spmd(nc, [arrays], core_ids=[0])
    y = r.results[0]["out"]
    return y.reshape(B, HALVES, P, KC, TOK).transpose(0, 1, 4, 3, 2).reshape(B, SEQ, DIM)
```
